# Optimizing a Trainium2 kernel written in Bass

```python
import numpy as np
import jax
import jax.numpy as jnp

def _softmax(x, axis=-1):
    return jax.nn.softmax(x, axis=axis)

def _gelu(x):
    return jax.nn.gelu(x, approximate=True)

def _silu(x):
    return jax.nn.silu(x)

def _sigmoid(x):
    return jax.nn.sigmoid(x)

def _layernorm(x, axis=-1, eps=1e-05):
    m = jnp.mean(x, axis=axis, keepdims=True)
    v = jnp.var(x, axis=axis, keepdims=True)
    return (x - m) / jnp.sqrt(v + eps)

def _scatter_add(tgt, idx, src, axis=0):
    return tgt.at[idx].add(src)

def _segment_sum(src, seg, n):
    return jax.ops.segment_sum(src, seg, n)
kernel_name = 'mk_flamingo_gated_d4_seqx_r4_41350f'

def setup_inputs(seed: int=0):
    np.random.seed(seed)
    _w = jnp.asarray

    def _rec_inputs():
        import jax
        import jax.numpy as jnp
        _rk = jax.random.key(seed)
        x = -0.0003929 + 0.9999 * jax.random.normal(jax.random.fold_in(_rk, 1), (16, 256, 256), jnp.float32)
        _lenS = 256 - jax.random.randint(jax.random.fold_in(_rk, 7), (16,), 0, max(1, 256 // 4) + 1, jnp.int32)
        _lenS2 = 256 - jax.random.randint(jax.random.fold_in(_rk, 8), (16,), 0, max(1, 256 // 4) + 1, jnp.int32)
        _ctx_1024P = jax.random.normal(jax.random.fold_in(_rk, 11), (16, 16, 256), jnp.float32)
        _ctx_1024c = jax.random.dirichlet(jax.random.fold_in(_rk, 511), 0.3 * jnp.ones((16,), jnp.float32), (16, 256))
        _ctx_1024t = jnp.einsum('bsk,bkd->bsd', _ctx_1024c, _ctx_1024P)
        _ctx_1024t = _ctx_1024t * jax.lax.rsqrt(jnp.mean(jnp.square(_ctx_1024t)) + 1e-12) * 0.953939
        ctx_1024 = 2.81802e-05 + 1.00001 * (_ctx_1024t + 0.3 * jax.random.normal(jax.random.fold_in(_rk, 611), (16, 256, 256), jnp.float32))
        _validS = jnp.arange(256)[None, :] < _lenS[:, None]
        _validS2 = jnp.arange(256)[None, :] < _lenS2[:, None]
        _causal = jnp.tril(jnp.ones((256, 256), dtype=bool))
        mask_BxS2_bk0 = jnp.logical_not(jnp.broadcast_to(_validS2[:, :], (16, 256)))
        _g = jax.random.normal(jax.random.fold_in(_rk, 9001), (2, 4), jnp.float32)
        _g = jnp.sign(_g) * jnp.maximum(jnp.abs(_g), 1.0) + (_g == 0) * 1.0
        g_xattn = _g[0]
        g_ffn = _g[1]
        return (x, ctx_1024, mask_BxS2_bk0, g_xattn, g_ffn)
    x, ctx_1024, mask_BxS2_bk0, g_xattn, g_ffn = _rec_inputs()

    def _L0_xattn_setup():
        import jax, jax.numpy as jnp
        import numpy as np
        EMBED = 256
        B, I, J = (8, 512, 512)
        SCALE = EMBED ** (-0.5)
        key = jax.random.key(seed)
        ks = jax.random.split(key, 5)
        s = EMBED ** (-0.5)
        return {'q_in': jax.random.normal(ks[0], (B, I, EMBED), dtype=jnp.float32), 'k_v': jax.random.normal(ks[1], (B, J, EMBED), dtype=jnp.float32), 'Wq': jax.random.normal(ks[2], (EMBED, EMBED), dtype=jnp.float32) * s, 'bq': jnp.zeros((EMBED,), dtype=jnp.float32), 'Wk': jax.random.normal(ks[3], (EMBED, EMBED), dtype=jnp.float32) * s, 'bk': jnp.zeros((EMBED,), dtype=jnp.float32), 'Wv': jax.random.normal(ks[4], (EMBED, EMBED), dtype=jnp.float32) * s, 'bv': jnp.zeros((EMBED,), dtype=jnp.float32)}
    _L0_xattn_all = _L0_xattn_setup()
    _L0_xattn_in = {k: v for k, v in _L0_xattn_all.items() if k in ('Wq', 'bq', 'Wk', 'bk', 'Wv', 'bv')}
    del _L0_xattn_all

    def _L0_ffn_setup():
        import jax, jax.numpy as jnp
        import numpy as np
        B, S, D, H, M, E, K = (4, 256, 256, 16, 2, 8, 2)
        KD = D // H
        F = 2 * D
        EPS = 1e-06

        def _ln(x, g, b):
            m = jnp.mean(x, axis=-1, keepdims=True)
            v = jnp.mean(jnp.square(x - m), axis=-1, keepdims=True)
            return (x - m) * jax.lax.rsqrt(v + EPS) * g + b
        key = jax.random.key(seed)
        ks = jax.random.split(key, 12)
        r = lambda i, shape: jax.random.normal(ks[i], shape, jnp.float32) * 0.02
        return {'x': jax.random.normal(ks[0], (B, S, D), jnp.float32), 'ln1_g': jnp.ones((D,), jnp.float32), 'ln1_b': jnp.zeros((D,), jnp.float32), 'ln2_g': jnp.ones((D,), jnp.float32), 'ln2_b': jnp.zeros((D,), jnp.float32), 'mha_wq': r(1, (M, D, H, KD)), 'mha_bq': jnp.zeros((M, H, KD), jnp.float32), 'mha_wk': r(2, (M, D, H, KD)), 'mha_bk': jnp.zeros((M, H, KD), jnp.float32), 'mha_wv': r(3, (M, D, H, KD)), 'mha_bv': jnp.zeros((M, H, KD), jnp.float32), 'mha_wo': r(4, (M, H, KD, D)), 'mha_bo': jnp.zeros((M, D), jnp.float32), 'mha_rw': r(5, (D, M)), 'mha_rb': jnp.zeros((M,), jnp.float32), 'ffn_rw': r(6, (D, E)), 'ffn_rb': jnp.zeros((E,), jnp.float32), 'fw1': r(7, (E, D, F)), 'fw2': r(8, (E, F, D))}
    _L0_ffn_all = _L0_ffn_setup()
    _L0_ffn_in = {k: v for k, v in _L0_ffn_all.items() if k in ('ln1_g', 'ln1_b', 'ln2_g', 'ln2_b', 'mha_wq', 'mha_bq', 'mha_wk', 'mha_bk', 'mha_wv', 'mha_bv', 'mha_wo', 'mha_bo', 'mha_rw', 'mha_rb', 'ffn_rw', 'ffn_rb', 'fw1', 'fw2')}
    del _L0_ffn_all

    def _L1_xattn_setup():
        import jax, jax.numpy as jnp
        import numpy as np
        import math
        D_MODEL = 256
        N_HEADS = 16
        C = 1
        B, L = (8, 512)

        def _glorot(key, fan):
            lim = np.sqrt(6.0 / (fan + fan)).astype(np.float32)
            return jax.random.uniform(key, (fan, fan), jnp.float32, -lim, lim)
        key = jax.random.key(seed)
        ks = jax.random.split(key, 7)
        queries = jax.random.normal(ks[0], (B, L, D_MODEL), jnp.float32)
        keys = jax.random.normal(ks[1], (B, L, D_MODEL), jnp.float32)
        values = jax.random.normal(ks[2], (B, L, D_MODEL), jnp.float32)
        wq = _glorot(ks[3], D_MODEL)
        wk = _glorot(ks[4], D_MODEL)
        wv = _glorot(ks[5], D_MODEL)
        wo = _glorot(ks[6], D_MODEL)
        return {'queries': queries, 'keys': keys, 'values': values, 'wq': wq, 'wk': wk, 'wv': wv, 'wo': wo}
    _L1_xattn_all = _L1_xattn_setup()
    _L1_xattn_in = {k: v for k, v in _L1_xattn_all.items() if k in ('wq', 'wk', 'wv', 'wo')}
    del _L1_xattn_all

    def _L1_ffn_setup():
        import jax, jax.numpy as jnp
        import numpy as np
        TOP_K = 2
        N_GROUP = 4
        TOPK_GROUP = 2
        ROUTED_SCALE = 2.5

        def _gate(xf, gate_w, gate_bias):
            logits = xf.astype(jnp.float32) @ gate_w.astype(jnp.float32)
            scores = jax.nn.sigmoid(logits)
            sfc = scores + gate_bias.astype(jnp.float32)[None]
            T, E = sfc.shape
            e_g = E // N_GROUP
            group_feat = sfc.reshape(T, N_GROUP, e_g)
            group_scores = jax.lax.top_k(group_feat, 2)[0].sum(axis=-1)
            _, group_idx = jax.lax.top_k(group_scores, TOPK_GROUP)
            group_mask = jax.nn.one_hot(group_idx, N_GROUP, dtype=sfc.dtype).sum(axis=1)
            score_mask = jnp.broadcast_to(group_mask[..., None], (T, N_GROUP, e_g)).reshape(T, E)
            tmp_scores = jnp.where(score_mask > 0, sfc, 0.0)
            _, topk_idx = jax.lax.top_k(tmp_scores, TOP_K)
            topk_w = jnp.take_along_axis(sfc, topk_idx, axis=-1)
            topk_w = topk_w / (topk_w.sum(axis=-1, keepdims=True) + 1e-20)
            return (topk_idx, topk_w * ROUTED_SCALE)
        key = jax.random.key(seed)
        ks = jax.random.split(key, 9)
        B, N, H, I, E, SH_I = (2, 256, 256, 128, 8, 256)
        s = lambda k, shape, scale: jax.random.normal(k, shape, jnp.float32) * scale
        return {'x': s(ks[0], (B, N, H), 1.0), 'gate_w': s(ks[1], (H, E), 0.02), 'gate_bias': s(ks[2], (E,), 0.02), 'w_gate': s(ks[3], (E, H, I), 0.02), 'w_up': s(ks[4], (E, H, I), 0.02), 'w_down': s(ks[5], (E, I, H), 0.02), 'sw_gate': s(ks[6], (H, SH_I), 0.02), 'sw_up': s(ks[7], (H, SH_I), 0.02), 'sw_down': s(ks[8], (SH_I, H), 0.02)}
    _L1_ffn_all = _L1_ffn_setup()
    _L1_ffn_in = {k: v for k, v in _L1_ffn_all.items() if k in ('gate_w', 'gate_bias', 'w_gate', 'w_up', 'w_down', 'sw_gate', 'sw_up', 'sw_down')}
    del _L1_ffn_all

    def _L2_xattn_setup():
        import jax, jax.numpy as jnp
        import numpy as np
        NUM_HEADS = 16
        key = jax.random.key(seed)
        ks = jax.random.split(key, 7)
        B, Nq, Nkv, D = (4, 256, 1024, 256)
        q = jax.random.normal(ks[0], (B, Nq, D), dtype=jnp.float32)
        kv = jax.random.normal(ks[1], (B, Nkv, D), dtype=jnp.float32)
        mask = jax.random.randint(ks[2], (B, Nkv), 0, 2) > 0
        mask = mask.at[:, 0].set(False)
        s = D ** (-0.5)
        Wq = jax.random.normal(ks[3], (D, D), dtype=jnp.float32) * s
        Wkv = jax.random.normal(ks[4], (D, 2 * D), dtype=jnp.float32) * s
        Wproj = jax.random.normal(ks[5], (D, D), dtype=jnp.float32) * s
        bproj = jnp.zeros((D,), dtype=jnp.float32)
        return {'q': q, 'kv': kv, 'key_padding_mask': mask, 'Wq': Wq, 'Wkv': Wkv, 'Wproj': Wproj, 'bproj': bproj}
    _L2_xattn_all = _L2_xattn_setup()
    _L2_xattn_in = {k: v for k, v in _L2_xattn_all.items() if k in ('Wq', 'Wkv', 'Wproj', 'bproj')}
    del _L2_xattn_all

    def _L2_ffn_setup():
        import jax, jax.numpy as jnp
        import numpy as np
        MICRO_BATCHES = 2
        TOP_K = 2
        LN_EPS = 1e-05
        B, S, D = (4, 1024, 256)
        E = 8
        DFF = 4 * D

        def _layernorm(x, g, b):
            mu = jnp.mean(x, axis=-1, keepdims=True)
            var = jnp.mean(jnp.square(x - mu), axis=-1, keepdims=True)
            return (x - mu) * jax.lax.rsqrt(var + LN_EPS) * g + b
        key = jax.random.key(seed)
        ks = jax.random.split(key, 12)
        sd = 1.0 / np.sqrt(D)
        sf = 1.0 / np.sqrt(DFF)
        return {'x': jax.random.normal(ks[0], (B, S, D), dtype=jnp.float32), 'ln_g': jnp.ones((D,), jnp.float32), 'ln_b': jnp.zeros((D,), jnp.float32), 'attn_w': jax.random.normal(ks[1], (D, D), jnp.float32) * sd, 'attn_b': jnp.zeros((D,), jnp.float32), 'gate_w': jax.random.normal(ks[2], (D, E), jnp.float32) * sd, 'w1': jax.random.normal(ks[3], (E, D, DFF), jnp.float32) * sd, 'b1': jnp.zeros((E, DFF), jnp.float32), 'w2': jax.random.normal(ks[4], (E, DFF, D), jnp.float32) * sf, 'b2': jnp.zeros((E, D), jnp.float32), 'next_w': jax.random.normal(ks[5], (D, D), jnp.float32) * sd, 'next_b': jnp.zeros((D,), jnp.float32)}
    _L2_ffn_all = _L2_ffn_setup()
    _L2_ffn_in = {k: v for k, v in _L2_ffn_all.items() if k in ('ln_g', 'ln_b', 'attn_w', 'attn_b', 'gate_w', 'w1', 'b1', 'w2', 'b2', 'next_w', 'next_b')}
    del _L2_ffn_all

    def _L3_xattn_setup():
        import jax, jax.numpy as jnp
        import numpy as np
        B, L, DM, H = (2, 1024, 256, 16)
        D = DM // H

        def _split_heads(x):
            b, l, _ = x.shape
            return x.reshape(b, l, H, D).transpose(0, 2, 1, 3)
        key = jax.random.key(seed)
        ks = jax.random.split(key, 11)
        s = 1.0 / np.sqrt(DM)
        return {'query': jax.random.normal(ks[0], (B, L, DM), jnp.float32), 'key': jax.random.normal(ks[1], (B, L, DM), jnp.float32), 'value': jax.random.normal(ks[2], (B, L, DM), jnp.float32), 'Wq': jax.random.normal(ks[3], (DM, DM), jnp.float32) * s, 'bq': jnp.zeros((DM,), jnp.float32), 'Wk': jax.random.normal(ks[4], (DM, DM), jnp.float32) * s, 'bk': jnp.zeros((DM,), jnp.float32), 'Wv': jax.random.normal(ks[5], (DM, DM), jnp.float32) * s, 'bv': jnp.zeros((DM,), jnp.float32), 'Wo': jax.random.normal(ks[6], (DM, DM), jnp.float32) * s, 'bo': jnp.zeros((DM,), jnp.float32)}
    _L3_xattn_all = _L3_xattn_setup()
    _L3_xattn_in = {k: v for k, v in _L3_xattn_all.items() if k in ('Wq', 'bq', 'Wk', 'bk', 'Wv', 'bv', 'Wo', 'bo')}
    del _L3_xattn_all

    def _L3_ffn_setup():
        import jax, jax.numpy as jnp
        import numpy as np
        D_MODEL = 256
        HIDDEN = 1024
        N_EXPERTS = 8
        TOP_K = 2
        key = jax.random.key(seed)
        k_x, k_r, k_w1, k_w2 = jax.random.split(key, 4)
        x = jax.random.normal(k_x, (2, 256, D_MODEL), dtype=jnp.float32)
        Wr = jax.random.normal(k_r, (D_MODEL, N_EXPERTS), dtype=jnp.float32) * 0.02
        W1 = jax.random.normal(k_w1, (N_EXPERTS, D_MODEL, HIDDEN), dtype=jnp.float32) * 0.02
        W2 = jax.random.normal(k_w2, (N_EXPERTS, HIDDEN, D_MODEL), dtype=jnp.float32) * 0.02
        return {'x': x, 'Wr': Wr, 'W1': W1, 'W2': W2}
    _L3_ffn_all = _L3_ffn_setup()
    _L3_ffn_in = {k: v for k, v in _L3_ffn_all.items() if k in ('Wr', 'W1', 'W2')}
    del _L3_ffn_all
    return {'x': x, 'ctx_1024': ctx_1024, 'mask_BxS2_bk0': mask_BxS2_bk0, 'g_xattn': g_xattn, 'g_ffn': g_ffn, 'L0_xattn_Wq': _L0_xattn_in['Wq'], 'L0_xattn_bq': _L0_xattn_in['bq'], 'L0_xattn_Wk': _L0_xattn_in['Wk'], 'L0_xattn_bk': _L0_xattn_in['bk'], 'L0_xattn_Wv': _L0_xattn_in['Wv'], 'L0_xattn_bv': _L0_xattn_in['bv'], 'L0_ffn_ln1_g': _L0_ffn_in['ln1_g'], 'L0_ffn_ln1_b': _L0_ffn_in['ln1_b'], 'L0_ffn_ln2_g': _L0_ffn_in['ln2_g'], 'L0_ffn_ln2_b': _L0_ffn_in['ln2_b'], 'L0_ffn_mha_wq': _L0_ffn_in['mha_wq'], 'L0_ffn_mha_bq': _L0_ffn_in['mha_bq'], 'L0_ffn_mha_wk': _L0_ffn_in['mha_wk'], 'L0_ffn_mha_bk': _L0_ffn_in['mha_bk'], 'L0_ffn_mha_wv': _L0_ffn_in['mha_wv'], 'L0_ffn_mha_bv': _L0_ffn_in['mha_bv'], 'L0_ffn_mha_wo': _L0_ffn_in['mha_wo'], 'L0_ffn_mha_bo': _L0_ffn_in['mha_bo'], 'L0_ffn_mha_rw': _L0_ffn_in['mha_rw'], 'L0_ffn_mha_rb': _L0_ffn_in['mha_rb'], 'L0_ffn_ffn_rw': _L0_ffn_in['ffn_rw'], 'L0_ffn_ffn_rb': _L0_ffn_in['ffn_rb'], 'L0_ffn_fw1': _L0_ffn_in['fw1'], 'L0_ffn_fw2': _L0_ffn_in['fw2'], 'L1_xattn_wq': _L1_xattn_in['wq'], 'L1_xattn_wk': _L1_xattn_in['wk'], 'L1_xattn_wv': _L1_xattn_in['wv'], 'L1_xattn_wo': _L1_xattn_in['wo'], 'L1_ffn_gate_w': _L1_ffn_in['gate_w'], 'L1_ffn_gate_bias': _L1_ffn_in['gate_bias'], 'L1_ffn_w_gate': _L1_ffn_in['w_gate'], 'L1_ffn_w_up': _L1_ffn_in['w_up'], 'L1_ffn_w_down': _L1_ffn_in['w_down'], 'L1_ffn_sw_gate': _L1_ffn_in['sw_gate'], 'L1_ffn_sw_up': _L1_ffn_in['sw_up'], 'L1_ffn_sw_down': _L1_ffn_in['sw_down'], 'L2_xattn_Wq': _L2_xattn_in['Wq'], 'L2_xattn_Wkv': _L2_xattn_in['Wkv'], 'L2_xattn_Wproj': _L2_xattn_in['Wproj'], 'L2_xattn_bproj': _L2_xattn_in['bproj'], 'L2_ffn_ln_g': _L2_ffn_in['ln_g'], 'L2_ffn_ln_b': _L2_ffn_in['ln_b'], 'L2_ffn_attn_w': _L2_ffn_in['attn_w'], 'L2_ffn_attn_b': _L2_ffn_in['attn_b'], 'L2_ffn_gate_w': _L2_ffn_in['gate_w'], 'L2_ffn_w1': _L2_ffn_in['w1'], 'L2_ffn_b1': _L2_ffn_in['b1'], 'L2_ffn_w2': _L2_ffn_in['w2'], 'L2_ffn_b2': _L2_ffn_in['b2'], 'L2_ffn_next_w': _L2_ffn_in['next_w'], 'L2_ffn_next_b': _L2_ffn_in['next_b'], 'L3_xattn_Wq': _L3_xattn_in['Wq'], 'L3_xattn_bq': _L3_xattn_in['bq'], 'L3_xattn_Wk': _L3_xattn_in['Wk'], 'L3_xattn_bk': _L3_xattn_in['bk'], 'L3_xattn_Wv': _L3_xattn_in['Wv'], 'L3_xattn_bv': _L3_xattn_in['bv'], 'L3_xattn_Wo': _L3_xattn_in['Wo'], 'L3_xattn_bo': _L3_xattn_in['bo'], 'L3_ffn_Wr': _L3_ffn_in['Wr'], 'L3_ffn_W1': _L3_ffn_in['W1'], 'L3_ffn_W2': _L3_ffn_in['W2']}

def reference(x, ctx_1024, mask_BxS2_bk0, g_xattn, g_ffn, L0_xattn_Wq, L0_xattn_bq, L0_xattn_Wk, L0_xattn_bk, L0_xattn_Wv, L0_xattn_bv, L0_ffn_ln1_g, L0_ffn_ln1_b, L0_ffn_ln2_g, L0_ffn_ln2_b, L0_ffn_mha_wq, L0_ffn_mha_bq, L0_ffn_mha_wk, L0_ffn_mha_bk, L0_ffn_mha_wv, L0_ffn_mha_bv, L0_ffn_mha_wo, L0_ffn_mha_bo, L0_ffn_mha_rw, L0_ffn_mha_rb, L0_ffn_ffn_rw, L0_ffn_ffn_rb, L0_ffn_fw1, L0_ffn_fw2, L1_xattn_wq, L1_xattn_wk, L1_xattn_wv, L1_xattn_wo, L1_ffn_gate_w, L1_ffn_gate_bias, L1_ffn_w_gate, L1_ffn_w_up, L1_ffn_w_down, L1_ffn_sw_gate, L1_ffn_sw_up, L1_ffn_sw_down, L2_xattn_Wq, L2_xattn_Wkv, L2_xattn_Wproj, L2_xattn_bproj, L2_ffn_ln_g, L2_ffn_ln_b, L2_ffn_attn_w, L2_ffn_attn_b, L2_ffn_gate_w, L2_ffn_w1, L2_ffn_b1, L2_ffn_w2, L2_ffn_b2, L2_ffn_next_w, L2_ffn_next_b, L3_xattn_Wq, L3_xattn_bq, L3_xattn_Wk, L3_xattn_bk, L3_xattn_Wv, L3_xattn_bv, L3_xattn_Wo, L3_xattn_bo, L3_ffn_Wr, L3_ffn_W1, L3_ffn_W2):
    import jax
    import jax.numpy as jnp

    def _L0_xattn_ref(q_in, k_v, Wq, bq, Wk, bk, Wv, bv):
        import jax, jax.numpy as jnp
        import numpy as np
        EMBED = 256
        B, I, J = (8, 512, 512)
        SCALE = EMBED ** (-0.5)
        q = q_in @ Wq + bq
        k = k_v @ Wk + bk
        v = k_v @ Wv + bv
        sim = jnp.einsum('bid,bjd->bij', q, k) * SCALE
        attn = jax.nn.softmax(sim, axis=-1)
        out = jnp.einsum('bij,bjd->bid', attn, v)
        return out

    def _L0_ffn_ref(x, ln1_g, ln1_b, ln2_g, ln2_b, mha_wq, mha_bq, mha_wk, mha_bk, mha_wv, mha_bv, mha_wo, mha_bo, mha_rw, mha_rb, ffn_rw, ffn_rb, fw1, fw2):
        import jax, jax.numpy as jnp
        import numpy as np
        B, S, D, H, M, E, K = (4, 256, 256, 16, 2, 8, 2)
        KD = D // H
        F = 2 * D
        EPS = 1e-06

        def _ln(x, g, b):
            m = jnp.mean(x, axis=-1, keepdims=True)
            v = jnp.mean(jnp.square(x - m), axis=-1, keepdims=True)
            return (x - m) * jax.lax.rsqrt(v + EPS) * g + b
        n1 = _ln(x, ln1_g, ln1_b)
        mha_probs = jax.nn.softmax(jnp.mean(n1, axis=1) @ mha_rw + mha_rb, axis=-1)
        q = jnp.einsum('btd,mdhk->mbhtk', n1, mha_wq) + mha_bq[:, None, :, None, :]
        kk = jnp.einsum('btd,mdhk->mbhtk', n1, mha_wk) + mha_bk[:, None, :, None, :]
        v = jnp.einsum('btd,mdhk->mbhtk', n1, mha_wv) + mha_bv[:, None, :, None, :]
        scores = jnp.einsum('mbhtk,mbhsk->mbhts', q, kk) / jnp.sqrt(jnp.float32(KD))
        attn = jax.nn.softmax(scores, axis=-1)
        ctx = jnp.einsum('mbhts,mbhsk->mbthk', attn, v)
        mha_out = jnp.einsum('mbthk,mhkd->mbtd', ctx, mha_wo) + mha_bo[:, None, None, :]
        x = x + jnp.einsum('mbtd,bm->btd', mha_out, mha_probs)
        n2 = _ln(x, ln2_g, ln2_b)
        ffn_probs = jax.nn.softmax(jnp.mean(n2, axis=1) @ ffn_rw + ffn_rb, axis=-1)
        topk_p, topk_i = jax.lax.top_k(ffn_probs, K)
        topk_p = topk_p / jnp.sum(topk_p, axis=-1, keepdims=True)
        sw1 = fw1[topk_i]
        sw2 = fw2[topk_i]
        h = jax.nn.gelu(jnp.einsum('btd,bkdf->bktf', n2, sw1), approximate=False)
        eo = jnp.einsum('bktf,bkfd->bktd', h, sw2)
        return x + jnp.einsum('bktd,bk->btd', eo, topk_p)

    def _L1_xattn_ref(queries, keys, values, wq, wk, wv, wo):
        import jax, jax.numpy as jnp
        import numpy as np
        import math
        D_MODEL = 256
        N_HEADS = 16
        C = 1
        B, L = (8, 512)

        def _glorot(key, fan):
            lim = np.sqrt(6.0 / (fan + fan)).astype(np.float32)
            return jax.random.uniform(key, (fan, fan), jnp.float32, -lim, lim)
        Bv, Lv, _ = queries.shape
        H = N_HEADS
        Dh = D_MODEL // N_HEADS
        Q = (queries @ wq).reshape(Bv, Lv, H, Dh).transpose(0, 2, 3, 1)
        K = (keys @ wk).reshape(Bv, Lv, H, Dh).transpose(0, 2, 3, 1)
        V = (values @ wv).reshape(Bv, Lv, H, Dh).transpose(0, 2, 3, 1)
        corr = jnp.fft.irfft(jnp.fft.rfft(Q, axis=-1) * jnp.conj(jnp.fft.rfft(K, axis=-1)), n=Lv, axis=-1)
        k_top = int(math.floor(C * math.log(Lv)))
        top_vals, top_idx = jax.lax.top_k(corr, k_top)
        w = jax.nn.softmax(top_vals, axis=-1)
        t = jnp.arange(Dh)
        out = jnp.zeros_like(V)
        for i in range(k_top):
            gather_idx = (t[None, None, :] - top_idx[..., i]) % Dh
            rolled = jnp.take_along_axis(V, gather_idx[..., None], axis=2)
            out = out + w[..., i, None] * rolled
        out = out.transpose(0, 2, 1, 3).reshape(Bv, Lv, D_MODEL)
        return out @ wo

    def _L1_ffn_ref(x, gate_w, gate_bias, w_gate, w_up, w_down, sw_gate, sw_up, sw_down):
        import jax, jax.numpy as jnp
        import numpy as np
        TOP_K = 2
        N_GROUP = 4
        TOPK_GROUP = 2
        ROUTED_SCALE = 2.5

        def _gate(xf, gate_w, gate_bias):
            logits = xf.astype(jnp.float32) @ gate_w.astype(jnp.float32)
            scores = jax.nn.sigmoid(logits)
            sfc = scores + gate_bias.astype(jnp.float32)[None]
            T, E = sfc.shape
            e_g = E // N_GROUP
            group_feat = sfc.reshape(T, N_GROUP, e_g)
            group_scores = jax.lax.top_k(group_feat, 2)[0].sum(axis=-1)
            _, group_idx = jax.lax.top_k(group_scores, TOPK_GROUP)
            group_mask = jax.nn.one_hot(group_idx, N_GROUP, dtype=sfc.dtype).sum(axis=1)
            score_mask = jnp.broadcast_to(group_mask[..., None], (T, N_GROUP, e_g)).reshape(T, E)
            tmp_scores = jnp.where(score_mask > 0, sfc, 0.0)
            _, topk_idx = jax.lax.top_k(tmp_scores, TOP_K)
            topk_w = jnp.take_along_axis(sfc, topk_idx, axis=-1)
            topk_w = topk_w / (topk_w.sum(axis=-1, keepdims=True) + 1e-20)
            return (topk_idx, topk_w * ROUTED_SCALE)
        B, N, H = x.shape
        xf = x.reshape(-1, H)
        topk_idx, topk_w = _gate(xf, gate_w, gate_bias)
        g = jax.nn.silu(jnp.einsum('th,ehi->tei', xf, w_gate))
        u = jnp.einsum('th,ehi->tei', xf, w_up)
        experts_y = jnp.einsum('tei,eih->teh', g * u, w_down)
        masked_y = jnp.take_along_axis(experts_y, topk_idx[:, :, None], axis=1)
        y = jnp.einsum('tkh,tk->th', masked_y, topk_w.astype(x.dtype)).reshape(B, N, H)
        shared = jax.nn.silu(x @ sw_gate) * (x @ sw_up) @ sw_down
        return y + shared

    def _L2_xattn_ref(q, kv, key_padding_mask, Wq, Wkv, Wproj, bproj):
        import jax, jax.numpy as jnp
        import numpy as np
        NUM_HEADS = 16
        B, Nq, D = q.shape
        Nkv = kv.shape[1]
        H = NUM_HEADS
        hd = D // H
        scale = hd ** (-0.5)
        qp = (q @ Wq).reshape(B, Nq, H, hd).transpose(0, 2, 1, 3) * scale
        kvp = kv @ Wkv
        k = kvp[..., :D].reshape(B, Nkv, H, hd).transpose(0, 2, 1, 3)
        v = kvp[..., D:].reshape(B, Nkv, H, hd).transpose(0, 2, 1, 3)
        attn = jnp.einsum('bhqd,bhkd->bhqk', qp, k)
        neg_inf = jnp.finfo(attn.dtype).min
        attn = jnp.where(key_padding_mask[:, None, None, :], neg_inf, attn)
        attn = jax.nn.softmax(attn, axis=-1)
        x = jnp.einsum('bhqk,bhkd->bhqd', attn, v)
        x = x.transpose(0, 2, 1, 3).reshape(B, Nq, D)
        return x @ Wproj + bproj

    def _L2_ffn_ref(x, ln_g, ln_b, attn_w, attn_b, gate_w, w1, b1, w2, b2, next_w, next_b):
        import jax, jax.numpy as jnp
        import numpy as np
        MICRO_BATCHES = 2
        TOP_K = 2
        LN_EPS = 1e-05
        B, S, D = (4, 1024, 256)
        E = 8
        DFF = 4 * D

        def _layernorm(x, g, b):
            mu = jnp.mean(x, axis=-1, keepdims=True)
            var = jnp.mean(jnp.square(x - mu), axis=-1, keepdims=True)
            return (x - mu) * jax.lax.rsqrt(var + LN_EPS) * g + b
        Bx, Sx, Dx = x.shape
        N = Bx * Sx
        x_flat = x.reshape(N, Dx)
        x_attn = _layernorm(x_flat, ln_g, ln_b) @ attn_w + attn_b + x_flat
        logits = x_attn @ gate_w
        _ = jax.lax.top_k(logits, TOP_K)
        tpe = N // (MICRO_BATCHES * E)
        g = x_attn.reshape(MICRO_BATCHES, E, tpe, Dx)
        h = jax.nn.gelu(jnp.einsum('metd,edf->metf', g, w1) + b1[None, :, None, :], approximate=False)
        y = jnp.einsum('metf,efd->metd', h, w2) + b2[None, :, None, :]
        out = jax.nn.gelu(y @ next_w + next_b, approximate=False)
        return out.reshape(Bx, Sx, Dx)

    def _L3_xattn_ref(query, key, value, Wq, bq, Wk, bk, Wv, bv, Wo, bo):
        import jax, jax.numpy as jnp
        import numpy as np
        B, L, DM, H = (2, 1024, 256, 16)
        D = DM // H

        def _split_heads(x):
            b, l, _ = x.shape
            return x.reshape(b, l, H, D).transpose(0, 2, 1, 3)
        q = _split_heads(query @ Wq + bq)
        k = _split_heads(key @ Wk + bk)
        v = _split_heads(value @ Wv + bv)
        q = jax.nn.elu(q) + 1.0
        k = jax.nn.elu(k) + 1.0
        S = jnp.einsum('bhle,bhld->bhed', k, q)
        out = jnp.einsum('bhme,bhed->bhmd', v, S)
        denom = jnp.einsum('bhld,bhld->bhl', q, k) + 1e-06
        out = out / denom[..., None]
        out = out.transpose(0, 2, 1, 3).reshape(out.shape[0], -1, DM)
        return out @ Wo + bo

    def _L3_ffn_ref(x, Wr, W1, W2):
        import jax, jax.numpy as jnp
        import numpy as np
        D_MODEL = 256
        HIDDEN = 1024
        N_EXPERTS = 8
        TOP_K = 2
        B, S, D = x.shape
        flat = x.reshape(-1, D)
        logits = flat @ Wr
        top_vals, top_idx = jax.lax.top_k(logits, TOP_K)
        weights = jax.nn.softmax(top_vals, axis=-1)
        top1 = top_idx[:, 0]
        w_top1 = weights[:, 0]
        h = jax.nn.gelu(jnp.einsum('td,edh->teh', flat, W1), approximate=False)
        y = jnp.einsum('teh,ehd->ted', h, W2)
        y_sel = jnp.take_along_axis(y, top1[:, None, None], axis=1)[:, 0, :]
        out = (w_top1[:, None] * y_sel).reshape(B, S, D)
        return out
    x = x + jnp.tanh(g_xattn[0]) * _L0_xattn_ref(_layernorm(x, axis=-1), ctx_1024, L0_xattn_Wq, L0_xattn_bq, L0_xattn_Wk, L0_xattn_bk, L0_xattn_Wv, L0_xattn_bv)
    x = x + jnp.tanh(g_ffn[0]) * _L0_ffn_ref(_layernorm(x, axis=-1), L0_ffn_ln1_g, L0_ffn_ln1_b, L0_ffn_ln2_g, L0_ffn_ln2_b, L0_ffn_mha_wq, L0_ffn_mha_bq, L0_ffn_mha_wk, L0_ffn_mha_bk, L0_ffn_mha_wv, L0_ffn_mha_bv, L0_ffn_mha_wo, L0_ffn_mha_bo, L0_ffn_mha_rw, L0_ffn_mha_rb, L0_ffn_ffn_rw, L0_ffn_ffn_rb, L0_ffn_fw1, L0_ffn_fw2)
    x = x + jnp.tanh(g_xattn[1]) * _L1_xattn_ref(_layernorm(x, axis=-1), ctx_1024, ctx_1024, L1_xattn_wq, L1_xattn_wk, L1_xattn_wv, L1_xattn_wo)
    x = x + jnp.tanh(g_ffn[1]) * _L1_ffn_ref(_layernorm(x, axis=-1), L1_ffn_gate_w, L1_ffn_gate_bias, L1_ffn_w_gate, L1_ffn_w_up, L1_ffn_w_down, L1_ffn_sw_gate, L1_ffn_sw_up, L1_ffn_sw_down)
    x = x + jnp.tanh(g_xattn[2]) * _L2_xattn_ref(_layernorm(x, axis=-1), ctx_1024, mask_BxS2_bk0, L2_xattn_Wq, L2_xattn_Wkv, L2_xattn_Wproj, L2_xattn_bproj)
    x = x + jnp.tanh(g_ffn[2]) * _L2_ffn_ref(_layernorm(x, axis=-1), L2_ffn_ln_g, L2_ffn_ln_b, L2_ffn_attn_w, L2_ffn_attn_b, L2_ffn_gate_w, L2_ffn_w1, L2_ffn_b1, L2_ffn_w2, L2_ffn_b2, L2_ffn_next_w, L2_ffn_next_b)
    x = x + jnp.tanh(g_xattn[3]) * _L3_xattn_ref(_layernorm(x, axis=-1), ctx_1024, ctx_1024, L3_xattn_Wq, L3_xattn_bq, L3_xattn_Wk, L3_xattn_bk, L3_xattn_Wv, L3_xattn_bv, L3_xattn_Wo, L3_xattn_bo)
    x = x + jnp.tanh(g_ffn[3]) * _L3_ffn_ref(_layernorm(x, axis=-1), L3_ffn_Wr, L3_ffn_W1, L3_ffn_W2)
    return x

_drawn_inputs = setup_inputs


def setup_inputs(seed=0):
    import zlib

    import numpy as np

    out = dict(_drawn_inputs(seed))
    spreads = {'L0_xattn_bq': (0.0, 0.33),
     'L0_xattn_bk': (0.0, 2.0),
     'L0_xattn_bv': (0.0, 0.1),
     'L0_ffn_ln1_g': (1.0, 0.6),
     'L0_ffn_ln1_b': (0.0, 0.332),
     'L0_ffn_ln2_g': (1.0, 0.2),
     'L0_ffn_ln2_b': (0.0, 0.272),
     'L0_ffn_mha_bq': (0.0, 0.8),
     'L0_ffn_mha_bk': (0.0, 2.0),
     'L0_ffn_mha_bv': (0.0, 0.292),
     'L0_ffn_mha_bo': (0.0, 0.1),
     'L0_ffn_mha_rb': (0.0, 0.8),
     'L0_ffn_ffn_rb': (0.0, 0.1),
     'L2_xattn_bproj': (0.0, 2.0),
     'L2_ffn_ln_g': (1.0, 0.6),
     'L2_ffn_ln_b': (0.0, 2.0),
     'L2_ffn_attn_b': (0.0, 2.0),
     'L2_ffn_b1': (0.0, 2.0),
     'L2_ffn_b2': (0.0, 1.979),
     'L2_ffn_next_b': (0.0, 2.0),
     'L3_xattn_bq': (0.0, 0.1),
     'L3_xattn_bk': (0.0, 0.1),
     'L3_xattn_bv': (0.0, 0.1),
     'L3_xattn_bo': (0.0, 2.0)}
    factors = {'g_ffn': 8.0,
     'L0_ffn_mha_wq': 8.0,
     'L0_ffn_mha_wk': 8.0,
     'L1_ffn_gate_w': 8.0,
     'L1_ffn_gate_bias': 8.0,
     'L1_ffn_w_gate': 8.0,
     'L1_ffn_w_up': 8.0,
     'L1_ffn_w_down': 8.0,
     'L1_ffn_sw_gate': 8.0,
     'L1_ffn_sw_up': 8.0,
     'L1_ffn_sw_down': 8.0,
     'L3_ffn_Wr': 8.0,
     'L3_ffn_W1': 8.0,
     'L3_ffn_W2': 8.0,
     'L2_xattn_Wq': 8.0,
     'L2_xattn_Wkv': 3.255,
     'L2_xattn_Wproj': 3.101,
     'L2_ffn_attn_w': 3.255,
     'L2_ffn_w1': 2.832}
    for name, (base, spread) in spreads.items():
        noise = np.random.default_rng([zlib.crc32(name.encode()), seed]).standard_normal(out[name].shape)
        drawn = base * np.exp(spread * noise) if base else spread * noise
        out[name] = jnp.asarray(drawn.astype(out[name].dtype))
    for name, factor in factors.items():
        out[name] = (out[name] * factor).astype(out[name].dtype)
    return out
```

```python
from contextlib import ExitStack

import concourse.bass as bass
from concourse import mybir

ALU = mybir.AluOpType
ACT = mybir.ActivationFunctionType
AX = mybir.AxisListType
F32 = mybir.dt.float32
BF16 = mybir.dt.bfloat16
U8 = mybir.dt.uint8
U32 = mybir.dt.uint32
I32 = mybir.dt.int32

P = 128
B = 16
S = 256
D = 256
C = D // P
H = 16
KD = D // H
NI = B // 2


class Chain:

    def __init__(self, eng, sem):
        self.eng, self.sem, self.k, self.base = eng, sem, 0, 0

    def start(self, base=0):
        self.k, self.base = 0, base

    def link(self, ins):
        self.k += 1
        ins.then_inc(self.sem, 1)
        self.eng.wait_ge(self.sem, self.base + self.k)

    def end(self, k):
        assert self.k == k, (self.k, k)


def passes(eng, body, n=NI):
    with eng.Fori(0, n - 1) as i:
        body(i, True)
    body(n - 1, False)


def nth(i, u):
    return 2 * i + u + 1


def product(pe, out, lhsT, rhs, K=C, M=C):
    for m in range(M):
        for k in range(K):
            last = pe.matmul(out(m), lhsT(k, m), rhs(k), start=(k == 0), stop=(k == K - 1))
    return last


def chunk(k):
    return slice(k * P, (k + 1) * P)


class Env:
    pass


def transpose4(pe, bank, src, ident):
    for dc in range(C):
        for tc in range(C):
            last = pe.transpose(bank[:, dc, chunk(tc)], src[:, tc, chunk(dc)], ident)
    return last


def ln_stats(v, ch, src, st, mv, scrap):
    for c in range(C):
        ins = v.bn_stats(st[:, c, :], src[:, c, :])
    ch.link(ins)
    v.memset(scrap[:], 0.0)
    for c in range(C):
        ins = v.bn_aggr(mv[:, c, :], st[:, c, :])
    return ins


def ln_rstd(g, ch, mv, rstd, mhalf, eps):
    ch.link(g.tensor_tensor(rstd[:, :], mv[:, :, 1], eps[:, 0:C], ALU.add))
    return g.tensor_tensor(rstd[:, :], rstd[:, :], mhalf[:, 0:C], ALU.pow)


def ln_apply(v, dst, src, mv, rstd):
    for c in range(C):
        ins = v.tensor_scalar(dst[:, c, :], src[:, c, :], mv[:, c, 0:1], rstd[:, c:c + 1],
                              ALU.subtract, ALU.mult)
    return ins


def load_weight(eng, dst, w, sem):
    eng.dma_start(dst, w.rearrange("(k p) n -> p k n", p=P)).then_inc(sem, 16)


def rows(ap1d):
    return ap1d.rearrange("(a n) -> a n", a=1).partition_broadcast(P)


def prepare(nc, env, w, sem_):
    with ExitStack() as ctx:
        sb = lambda n, s, d=F32: ctx.enter_context(nc.sbuf_tensor(n, s, d))
        gates = sb("gates", [P, 8])
        ctx_in = sb("ctx_in", [P, 4, C, D])
        ones = sb("ones", [P, P])
        ctx_ld = [sem_(f"ctx_ld{j}") for j in range(4)]
        x_in, gates_in, made, made_id, ctx_mm, ctx_ev = (
            sem_(n) for n in ("x_in", "gates_in", "made", "made_id", "ctx_mm", "ctx_ev"))
        block = ctx.enter_context(nc.Block())

        @block.sync
        def _(sp):
            sp.dma_start(gates[:, 0:4], rows(w["g_xattn"])).then_inc(gates_in, 16)
            sp.dma_start(gates[:, 4:8], rows(w["g_ffn"])).then_inc(gates_in, 16)
            xv = w["x"].rearrange("b (c p) d -> p b c d", p=P)
            cv = w["ctx_1024"].rearrange("b (c p) d -> p b c d", p=P)
            for b in range(B):
                if b >= 4:
                    sp.wait_ge(ctx_mm, b - 3)
                sp.dma_start(ctx_in[:, b % 4], cv[:, b]).then_inc(ctx_ld[b % 4], 16)
                sp.dma_start(env.x[:, b], xv[:, b]).then_inc(x_in, 16)
            sp.wait_ge(x_in, 16 * B)

        @block.gpsimd
        def _(g):
            g.memset(env.eps5[:], 1e-5).then_inc(made, 1)
            g.memset(env.eps6[:], 1e-6).then_inc(made, 1)
            g.memset(ones[:], 1.0).then_inc(made, 1)
            g.memset(env.mhalf[:], -0.5).then_inc(made, 1)
            g.wait_ge(made, 4)
            g.affine_select(out=env.ident[:], in_=ones[:], compare_op=ALU.is_equal, fill=0.0, base=0,
                            pattern=[[-1, P]], channel_multiplier=1).then_inc(made_id, 1)

        @block.scalar
        def _(a):
            a.wait_ge(gates_in, 32)
            a.activation(env.tg[:], gates[:], ACT.Tanh)

        @block.tensor
        def _(pe):
            pe.wait_ge(made_id, 1)
            for b in range(B):
                pe.wait_ge(ctx_ld[b % 4], 16 * (b // 4 + 1))
                if b >= 2:
                    pe.wait_ge(ctx_ev, b - 1)
                transpose4(pe, env.bank(b % 2), ctx_in[:, b % 4], env.ident[:]).then_inc(ctx_mm, 1)

        @block.vector
        def _(v):
            for b in range(B):
                v.wait_ge(ctx_mm, b + 1)
                v.tensor_copy(env.ctxT[:, b], env.bank(b % 2)).then_inc(ctx_ev, 1)


def layer0_attention(nc, env, w, sem_):
    scale = D ** -0.5
    with ExitStack() as ctx:
        sb = lambda n, s, d=F32: ctx.enter_context(nc.sbuf_tensor("A0" + n, s, d))
        wq, wk, wv = (sb(n, [P, C, D]) for n in ("wq", "wk", "wv"))
        bq, bk = (sb(n, [P, C]) for n in ("bq", "bk"))
        bv = sb("bv", [P, D])
        xn, xnT, cT, qT, kT, vt, pr, prT = (sb(n, [P, 2, C, D]) for n in
                                            ("xn", "xnT", "cT", "qT", "kT", "v", "pr", "prT"))
        st, mv, rstd = sb("st", [P, 2, C, 6]), sb("mv", [P, 2, C, 2]), sb("rstd", [P, 2, C])
        nm, rs, ri = sb("nm", [P, 2, C]), sb("rs", [P, 2, C]), sb("ri", [P, 2, C])
        (w_in, st_rdy, rstd_rdy, xn_rdy, xnT_mm, xnT_rdy, cT_rdy, q_mm, k_mm, v_mm, q_rdy, k_rdy, v_rdy,
         s_mm, nm_rdy, p_rdy, pT_mm, pT_rdy, o_mm, v_ch, g_ch) = (
            sem_("a0_" + n) for n in ("w_in", "st_rdy", "rstd_rdy", "xn_rdy", "xnT_mm", "xnT_rdy", "cT_rdy",
                                      "q_mm", "k_mm", "v_mm", "q_rdy", "k_rdy", "v_rdy", "s_mm", "nm_rdy",
                                      "p_rdy", "pT_mm", "pT_rdy", "o_mm", "v_ch", "g_ch"))
        bankA, bankB, bankC, bankD = ([env.bank(4 * u + j) for u in (0, 1)] for j in range(4))
        block = ctx.enter_context(nc.Block())

        @block.sync
        def _(sp):
            load_weight(sp, wq[:], w["L0_xattn_Wq"], w_in)
            load_weight(sp, wk[:], w["L0_xattn_Wk"], w_in)
            load_weight(sp, wv[:], w["L0_xattn_Wv"], w_in)
            sp.dma_start(bq[:], w["L0_xattn_bq"]).then_inc(w_in, 16)
            sp.dma_start(bk[:], w["L0_xattn_bk"]).then_inc(w_in, 16)
            sp.dma_start(bv[:], rows(w["L0_xattn_bv"])).then_inc(w_in, 16)

        @block.gpsimd
        def _(g):
            ch = Chain(g, g_ch)

            def front(i):
                ch.start(2 * i)
                for u in (0, 1):
                    g.wait_ge(st_rdy, nth(i, u))
                    ln_rstd(g, ch, mv[:, u], rstd[:, u], env.mhalf, env.eps5).then_inc(rstd_rdy, 1)
                ch.end(2)
                for u in (0, 1):
                    g.tensor_copy(cT[:, u], env.ctxT[:, 2 * i + u]).then_inc(cT_rdy, 1)

            front(0)

            def body(i, more):
                if more:
                    g.wait_ge(v_mm, nth(i, 1))
                    front(i + 1)
            passes(g, body)

        @block.vector
        def _(v):
            ch = Chain(v, v_ch)

            def front(i):
                for u in (0, 1):
                    ln_stats(v, ch, env.x[:, 2 * i + u], st[:, u], mv[:, u], env.scrap).then_inc(st_rdy, 1)
                for u in (0, 1):
                    v.wait_ge(rstd_rdy, nth(i, u))
                    ln_apply(v, xn[:, u], env.x[:, 2 * i + u], mv[:, u], rstd[:, u]).then_inc(xn_rdy, 1)

            front(0)

            def body(i, more):
                for u in (0, 1):
                    v.wait_ge(q_mm, nth(i, u))
                    if u == 0:
                        v.wait_ge(w_in, 96)
                    for c in range(C):
                        last = v.tensor_scalar(qT[:, u, c], bankB[u][:, c], bq[:, c:c + 1], scale,
                                               ALU.add, ALU.mult)
                    last.then_inc(q_rdy, 1)
                    v.wait_ge(v_mm, nth(i, u))
                    for c in range(C):
                        last = v.tensor_tensor(vt[:, u, c], bankA[u][:, c], bv[:], ALU.add)
                    last.then_inc(v_rdy, 1)
                for u in (0, 1):
                    v.wait_ge(s_mm, nth(i, u))
                    v.tensor_reduce(nm[:, u, :], bankB[u], AX.X, ALU.max, negate=True).then_inc(nm_rdy, 1)
                ch.start(6 * i + 2)
                if more:
                    front(i + 1)
                for u in (0, 1):
                    v.wait_ge(p_rdy, nth(i, u))
                    ch.link(v.reciprocal(ri[:, u], rs[:, u]))
                    ch.link(v.tensor_scalar(ri[:, u], ri[:, u], env.tg[:, 0:1], None, ALU.mult))
                    v.wait_ge(o_mm, nth(i, u))
                    for c in range(C):
                        v.scalar_tensor_tensor(
                            env.x[:, 2 * i + u, c], bankD[u][:, c], ri[:, u, c:c + 1],
                            env.x[:, 2 * i + u, c], ALU.mult, ALU.add)
            passes(v, body)

        @block.scalar
        def _(a):
            def front(i):
                for u in (0, 1):
                    a.wait_ge(xnT_mm, nth(i, u))
                    a.activation(xnT[:, u], bankA[u], ACT.Copy).then_inc(xnT_rdy, 1)

            front(0)

            def body(i, more):
                for u in (0, 1):
                    a.wait_ge(k_mm, nth(i, u))
                    for c in range(C):
                        last = a.activation(kT[:, u, c], bankC[u][:, c], ACT.Identity, bias=bk[:, c:c + 1])
                    last.then_inc(k_rdy, 1)
                for u in (0, 1):
                    a.wait_ge(nm_rdy, nth(i, u))
                    for c in range(C):
                        last = a.activation(pr[:, u, c], bankB[u][:, c], ACT.Exp, bias=nm[:, u, c:c + 1],
                                            accum_out=rs[:, u, c:c + 1])
                    last.then_inc(p_rdy, 1)
                if more:
                    front(i + 1)
                for u in (0, 1):
                    a.wait_ge(pT_mm, nth(i, u))
                    a.activation(prT[:, u], bankC[u], ACT.Copy).then_inc(pT_rdy, 1)
            passes(a, body)

        @block.tensor
        def _(pe):
            def front(i):
                for u in (0, 1):
                    pe.wait_ge(xn_rdy, nth(i, u))
                    transpose4(pe, bankA[u], xn[:, u], env.ident[:]).then_inc(xnT_mm, 1)

            front(0)
            pe.wait_ge(w_in, 96)

            def body(i, more):
                for u in (0, 1):
                    pe.wait_ge(xnT_rdy, nth(i, u))
                    product(pe, lambda m: bankB[u][:, m], lambda k, m: wq[:, k, chunk(m)],
                            lambda k: xnT[:, u, k]).then_inc(q_mm, 1)
                    pe.wait_ge(cT_rdy, nth(i, u))
                    product(pe, lambda m: bankC[u][:, m], lambda k, m: wk[:, k, chunk(m)],
                            lambda k: cT[:, u, k]).then_inc(k_mm, 1)
                    product(pe, lambda m: bankA[u][:, m], lambda k, m: cT[:, u, k, chunk(m)],
                            lambda k: wv[:, k]).then_inc(v_mm, 1)
                for u in (0, 1):
                    pe.wait_ge(q_rdy, nth(i, u))
                    pe.wait_ge(k_rdy, nth(i, u))
                    product(pe, lambda m: bankB[u][:, m], lambda k, m: qT[:, u, k, chunk(m)],
                            lambda k: kT[:, u, k]).then_inc(s_mm, 1)
                for u in (0, 1):
                    pe.wait_ge(v_rdy, nth(i, u))
                if more:
                    front(i + 1)
                for u in (0, 1):
                    pe.wait_ge(p_rdy, nth(i, u))
                    transpose4(pe, bankC[u], pr[:, u], env.ident[:]).then_inc(pT_mm, 1)
                for u in (0, 1):
                    pe.wait_ge(pT_rdy, nth(i, u))
                    product(pe, lambda m: bankD[u][:, m], lambda k, m: prT[:, u, k, chunk(m)],
                            lambda k: vt[:, u, k]).then_inc(o_mm, 1)
            passes(pe, body)


class Heads:

    STEPS = H + 3

    def __init__(self, nc, env, ctx, sem_, tag, masked=False):
        sb = lambda n, s, d=F32: ctx.enter_context(nc.sbuf_tensor(tag + n, s, d))
        self.env = env
        self.own = sb("own", [P, 8])
        self.qT, self.kT, self.vt = (sb(n, [P, C, S]) for n in ("hqT", "hkT", "hv"))
        self.qm = sb("hqm", [P, 3, S])
        self.pr, self.pT = sb("hpr", [P, 3, C, S]), sb("hpT", [P, 2, C, S])
        self.nm, self.rs, self.ri = sb("hnm", [P, H, C]), sb("hrs", [P, C, H]), sb("hri", [P, C, H])
        self.on = sb("hon", [P, C, D])
        self.scores = [env.bank(0), env.bank(1)]
        self.turned = [env.bank(2), env.bank(3)]
        self.out = env.bank(4)
        (self.qm_rdy, self.s_mm, self.nm_rdy, self.p_rdy, self.t_mm, self.tr_a, self.tr_v, self.av_mm) = (
            sem_(tag + n) for n in ("qm_rdy", "s_mm", "nm_rdy", "p_rdy", "t_mm", "tr_a", "tr_v", "av_mm"))
        self.masked = masked

    def mask(self, v, h):
        v.tensor_scalar(self.qm[:, h % 3], self.qT[:, h // 8], self.own[:, h % 8:h % 8 + 1], None,
                        ALU.mult).then_inc(self.qm_rdy, 1)

    def vector(self, v, job, mid):
        self.mask(v, 0)
        self.mask(v, 1)
        for st in range(self.STEPS):
            if st < H:
                v.wait_ge(self.s_mm, H * job + st + 1)
                v.tensor_reduce(self.nm[:, st], self.scores[st % 2], AX.X, ALU.max,
                                negate=True).then_inc(self.nm_rdy, 1)
                if st + 2 < H:
                    self.mask(v, st + 2)
            h = st - 2
            if 0 <= h < H and h % 2:
                v.wait_ge(self.t_mm, H * job + h + 1)
                v.tensor_copy(self.pT[:, 1], self.turned[1]).then_inc(self.tr_v, 1)
            if st in mid:
                mid[st]()

    def scalar(self, a, job, mid):
        for st in range(self.STEPS):
            if st < H:
                a.wait_ge(self.nm_rdy, H * job + st + 1)
                for c in range(C):
                    last = a.activation(self.pr[:, st % 3, c], self.scores[st % 2][:, c], ACT.Exp,
                                        bias=self.nm[:, st, c:c + 1], accum_out=self.rs[:, c, st:st + 1])
                last.then_inc(self.p_rdy, 1)
            h = st - 2
            if 0 <= h < H and h % 2 == 0:
                a.wait_ge(self.t_mm, H * job + h + 1)
                a.activation(self.pT[:, 0], self.turned[0], ACT.Copy).then_inc(self.tr_a, 1)
            if st in mid:
                mid[st]()

    def tensor(self, pe, job, mid, before_turn, mask=None):
        for st in range(self.STEPS):
            if st < H:
                h = st
                pe.wait_ge(self.qm_rdy, H * job + h + 1)
                if h >= 2:
                    pe.wait_ge(self.p_rdy, H * job + h - 1)
                bank = self.scores[h % 2]
                if self.masked:
                    mask(bank)
                for tc in range(C):
                    last = pe.matmul(bank[:, tc], self.qm[:, h % 3, chunk(tc)], self.kT[:, h // 8],
                                     start=not self.masked, stop=True, skip_group_check=self.masked)
                last.then_inc(self.s_mm, 1)
            h = st - 2
            if 0 <= h < H:
                if h == 0:
                    before_turn()
                pe.wait_ge(self.p_rdy, H * job + h + 1)
                if h >= 2:
                    pe.wait_ge(self.tr_v if h % 2 else self.tr_a, 8 * job + (h - 2) // 2 + 1)
                transpose4(pe, self.turned[h % 2], self.pr[:, h % 3], self.env.ident[:]).then_inc(self.t_mm, 1)
            h = st - 3
            if 0 <= h < H:
                pe.wait_ge(self.tr_v if h % 2 else self.tr_a, 8 * job + h // 2 + 1)
                for tc in range(C):
                    for sc in range(C):
                        last = pe.matmul(self.out[:, tc, h * KD:(h + 1) * KD], self.pT[:, h % 2, sc, chunk(tc)],
                                         self.vt[:, sc, h * KD:(h + 1) * KD], start=(sc == 0), stop=(sc == C - 1))
                last.then_inc(self.av_mm, 1)
            if st in mid:
                mid[st]()

    def normalise(self, v, ch, job, weight=None):
        v.wait_ge(self.av_mm, H * (job + 1))
        ch.link(v.reciprocal(self.ri[:], self.rs[:]))
        if weight is not None:
            ch.link(v.tensor_scalar(self.ri[:], self.ri[:], weight, None, ALU.mult))
        return v.tensor_tensor(self.on[:].rearrange("p c (h k) -> p (c h) k", k=KD),
                               self.out.rearrange("p c (h k) -> p (c h) k", k=KD),
                               self.ri[:].rearrange("p c h -> p (c h)").unsqueeze(2).broadcast_to([P, C * H, KD]),
                               ALU.mult)


def layer0_mha(nc, env, w, sem_):
    with ExitStack() as ctx:
        sb = lambda n, s, d=F32: ctx.enter_context(nc.sbuf_tensor("M0" + n, s, d))
        hd = Heads(nc, env, ctx, sem_, "m0")
        wq, wk, wv, wo = (sb(n, [P, 2, C, D]) for n in ("wq", "wk", "wv", "wo"))
        bq, bk = sb("bq", [P, 2, C]), sb("bk", [P, 2, C])
        bv, bo = sb("bv", [P, 2, D]), sb("bo", [P, 2, D])
        g1, b1, g2, b2 = (sb(n, [P, C]) for n in ("g1", "b1", "g2", "b2"))
        rw1, rb1, rw2, rb2 = sb("rw1", [P, C, 2]), sb("rb1", [P, 2]), sb("rw2", [P, C, 8]), sb("rb2", [P, 8])
        ones = sb("ones", [P, P])
        xn, nn, n1T, base, x1 = (sb(n, [P, C, D]) for n in ("xn", "nn", "n1T", "base", "x1"))
        onT = sb("onT", [P, 2, C, S])
        st, mv, rstd = sb("st", [P, C, 6]), sb("mv", [P, C, 2]), sb("rstd", [P, C])
        s1, sbr = sb("s1", [P, C]), sb("sbr", [P, C, P])
        z, nz, ez, es, ie = sb("z", [P, 8]), sb("nz", [P, 1]), sb("ez", [P, 8]), sb("es", [P, 1]), sb("ie", [P, 1])
        probs, probs_next, top = sb("probs", [P, 2]), sb("probs_next", [P, 2]), sb("top", [P, 8])
        absorb = sb("absorb", [P, 1])
        pb, ti, ts = sb("pb", [P, 8]), sb("ti", [P, 8], U32), sb("ts", [P, 1])
        (w_in, ones_rdy, st_rdy, rstd_rdy, nn_rdy, nT_mm, s_rdy, sb_rdy, lg_mm, z_rdy, e_rdy, q_mm, k_mm, v_mm,
         k_rdy, v_rdy, on_rdy, oT_mm, oT_rdy, mh_mm, v_ch, g_ch) = (
            sem_("m0_" + n) for n in (
                "w_in", "ones_rdy", "st_rdy", "rstd_rdy", "nn_rdy", "nT_mm", "s_rdy", "sb_rdy", "lg_mm", "z_rdy",
                "e_rdy", "q_mm", "k_mm", "v_mm", "k_rdy", "v_rdy", "on_rdy", "oT_mm", "oT_rdy", "mh_mm", "v_ch",
                "g_ch"))
        G0, G1, G2 = env.bank(5), env.bank(6), env.bank(7)
        loads = 23
        block = ctx.enter_context(nc.Block())

        @block.sync
        def _(sp):
            for t, name in ((wq, "wq"), (wk, "wk"), (wv, "wv")):
                for m in range(2):
                    src = w["L0_ffn_mha_" + name][m].rearrange("(k p) h n -> p k (h n)", p=P)
                    sp.dma_start(t[:, m], src).then_inc(w_in, 16)
            for m in range(2):
                src = w["L0_ffn_mha_wo"][m].rearrange("h k n -> (h k) n").rearrange("(c p) n -> p c n", p=P)
                sp.dma_start(wo[:, m], src).then_inc(w_in, 16)
                sp.dma_start(bv[:, m], rows(w["L0_ffn_mha_bv"][m].rearrange("h k -> (h k)"))).then_inc(w_in, 16)
                sp.dma_start(bo[:, m], rows(w["L0_ffn_mha_bo"][m])).then_inc(w_in, 16)
            sp.dma_start(bq[:], w["L0_ffn_mha_bq"].rearrange("p (m c) -> p m c", m=2)).then_inc(w_in, 16)
            sp.dma_start(bk[:], w["L0_ffn_mha_bk"].rearrange("p (m c) -> p m c", m=2)).then_inc(w_in, 16)
            for t, name in ((g1, "ln1_g"), (b1, "ln1_b"), (g2, "ln2_g"), (b2, "ln2_b")):
                sp.dma_start(t[:], w["L0_ffn_" + name]).then_inc(w_in, 16)
            sp.dma_start(rw1[:], w["L0_ffn_mha_rw"].rearrange("(k p) n -> p k n", p=P)).then_inc(w_in, 16)
            sp.dma_start(rw2[:], w["L0_ffn_ffn_rw"].rearrange("(k p) n -> p k n", p=P)).then_inc(w_in, 16)
            sp.dma_start(rb1[:], rows(w["L0_ffn_mha_rb"])).then_inc(w_in, 16)
            sp.dma_start(rb2[:], rows(w["L0_ffn_ffn_rb"])).then_inc(w_in, 16)
            sp.dma_start(hd.own[:], w["own"]).then_inc(w_in, 16)

        @block.gpsimd
        def _(g):
            ch = Chain(g, g_ch)
            g.memset(ones[:], 1.0).then_inc(ones_rdy, 1)

            def rstds(b, first, last):
                for j in range(first, last):
                    ch.start(3 * b + j)
                    g.wait_ge(st_rdy, 3 * b + j + 1)
                    ln_rstd(g, ch, mv[:], rstd[:], env.mhalf, env.eps5 if j == 0 else env.eps6).then_inc(rstd_rdy, 1)

            rstds(0, 0, 2)

            def body(b, more):
                if more:
                    g.wait_ge(st_rdy, 3 * b + 3)
                    ch.start(3 * b + 2)
                    ln_rstd(g, ch, mv[:], rstd[:], env.mhalf, env.eps5).then_inc(rstd_rdy, 1)
                    g.wait_ge(st_rdy, 3 * b + 4)
                    ch.start(3 * b + 3)
                    ln_rstd(g, ch, mv[:], rstd[:], env.mhalf, env.eps6).then_inc(rstd_rdy, 1)
                    g.wait_ge(st_rdy, 3 * b + 5)
                    ch.start(3 * b + 4)
                    ln_rstd(g, ch, mv[:], rstd[:], env.mhalf, env.eps6).then_inc(rstd_rdy, 1)
                else:
                    g.wait_ge(st_rdy, 3 * b + 3)
                    ch.start(3 * b + 2)
                    ln_rstd(g, ch, mv[:], rstd[:], env.mhalf, env.eps6).then_inc(rstd_rdy, 1)
            passes(g, body, B)

        @block.vector
        def _(v):
            ch = Chain(v, v_ch)

            def stats(src):
                ln_stats(v, ch, src, st, mv, env.scrap).then_inc(st_rdy, 1)

            def front_a(b):
                stats(env.x[:, b])

            def front_b(b, before):
                v.wait_ge(rstd_rdy, before + 1)
                ch.link(ln_apply(v, xn, env.x[:, b], mv, rstd))
                stats(xn)

            def front_c(before):
                v.wait_ge(rstd_rdy, before + 2)
                ln_apply(v, nn, xn, mv, rstd).then_inc(nn_rdy, 1)

            def spread(count):
                v.wait_ge(s_rdy, count)
                for k in range(C):
                    last = v.tensor_scalar(sbr[:, k], ones[:], s1[:, k:k + 1], None, ALU.mult)
                last.then_inc(sb_rdy, 1)

            def logits(count, n, rb):
                v.wait_ge(lg_mm, count)
                ch.link(v.scalar_tensor_tensor(z[:, 0:n], G2[:, 0, 0:n], 1.0 / S, rb[:, 0:n], ALU.mult, ALU.add))
                v.tensor_reduce(nz[:], z[:, 0:n], AX.X, ALU.max, negate=True).then_inc(z_rdy, 1)

            def finish(count, n, dst):
                v.wait_ge(e_rdy, count)
                ch.link(v.reciprocal(ie[:], es[:]))
                ch.link(v.tensor_scalar(dst[:, 0:n], ez[:, 0:n], ie[:, 0:1], None, ALU.mult))

            v.wait_ge(ones_rdy, 1)
            v.wait_ge(w_in, 16 * loads)
            ch.start(0)
            front_a(0)
            front_b(0, 0)
            front_c(0)
            spread(1)
            logits(1, 2, rb1)
            finish(1, 2, probs_next)
            ch.end(6)

            def body(b, more):
                ch.start(24 * b + 6)
                ch.link(v.tensor_copy(probs[:], probs_next[:]))
                for m, src in ((0, xn), (1, base)):
                    for c in range(C):
                        last = v.scalar_tensor_tensor(base[:, c], bo[:, m], probs[:, m:m + 1], src[:, c],
                                                      ALU.mult, ALU.add)
                    ch.link(last)
                for m in range(2):
                    v.wait_ge(q_mm, 2 * b + m + 1)
                    for c in range(C):
                        last = v.tensor_scalar(hd.qT[:, c], G0[:, c], bq[:, m, c:c + 1], KD ** -0.5,
                                               ALU.add, ALU.mult)
                    ch.link(last)
                    v.wait_ge(v_mm, 2 * b + m + 1)
                    for c in range(C):
                        last = v.tensor_tensor(hd.vt[:, c], G2[:, c], bv[:, m], ALU.add)
                    last.then_inc(v_rdy, 1)
                    mid = {}
                    if m == 1 and more:
                        mid = {3: lambda: front_a(b + 1), 6: lambda: front_b(b + 1, 3 * b + 2),
                               9: lambda: front_c(3 * b + 2), 14: lambda: spread(2 * b + 2),
                               16: lambda: logits(2 * b + 2, 2, rb1),
                               18: lambda: finish(2 * b + 2, 2, probs_next)}
                    hd.vector(v, 2 * b + m, mid)
                    hd.normalise(v, ch, 2 * b + m, probs[:, m:m + 1]).then_inc(on_rdy, 1)
                v.wait_ge(mh_mm, b + 1)
                ch.link(v.tensor_tensor(x1[:], G0, base[:], ALU.add))
                v.scalar_tensor_tensor(env.x[:, b], x1[:], env.tg[:, 4:5], env.x[:, b], ALU.mult, ALU.add)
                stats(x1)
                v.wait_ge(rstd_rdy, 3 * b + (5 if more else 3))
                ln_apply(v, nn, x1, mv, rstd).then_inc(nn_rdy, 1)
                count = 2 * b + (3 if more else 2)
                spread(count)
                logits(count, 8, rb2)
                finish(count, 8, pb)
                v.memset(env.scrap[:], 0.0)
                ch.link(v.max(top[:], pb[:]))
                v.memset(env.scrap[:], 0.0)
                v.max_index(ti[:], top[:], pb[:])
                ch.link(v.tensor_tensor(ts[:], top[:, 0:1], top[:, 1:2], ALU.add))
                ch.link(v.reciprocal(ts[:], ts[:]))
                ch.link(v.tensor_scalar(top[:, 0:2], top[:, 0:2], ts[:, 0:1], env.tg[:, 4:5], ALU.mult, ALU.mult))
                v.tensor_copy(env.pick_w[:, b], top[:, 0:2])
                v.tensor_copy(env.pick[:, b], ti[:, 0:2])
                if more:
                    ch.end(24)
            passes(v, body, B)

        @block.scalar
        def _(a):
            def turned(count, bank, dst, gain, bias):
                a.wait_ge(nT_mm, count)
                a.activation(absorb[:], env.eps5[:, 0:1], ACT.Copy)
                for k in range(C):
                    last = a.activation(dst[:, k], bank[:, k], ACT.Identity, scale=gain[:, k:k + 1],
                                        bias=bias[:, k:k + 1], accum_out=s1[:, k:k + 1])
                last.then_inc(s_rdy, 1)

            def router_exp(count, n):
                a.wait_ge(z_rdy, count)
                a.activation(ez[:, 0:n], z[:, 0:n], ACT.Exp, bias=nz[:, 0:1], accum_out=es[:]).then_inc(e_rdy, 1)

            a.wait_ge(w_in, 16 * loads)
            turned(1, G0, n1T, g1, b1)
            router_exp(1, 2)

            def body(b, more):
                for m in range(2):
                    a.wait_ge(k_mm, 2 * b + m + 1)
                    for c in range(C):
                        last = a.activation(hd.kT[:, c], G1[:, c], ACT.Identity, bias=bk[:, m, c:c + 1])
                    last.then_inc(k_rdy, 1)
                    if m == 1:
                        a.wait_ge(oT_mm, 2 * b + 1)
                        a.activation(onT[:, 0], hd.turned[0], ACT.Copy).then_inc(oT_rdy, 1)
                    mid = {}
                    if m == 1 and more:
                        mid = {13: lambda: turned(2 * b + 2, G0, n1T, g1, b1), 17: lambda: router_exp(2 * b + 2, 2)}
                    hd.scalar(a, 2 * b + m, mid)
                a.wait_ge(oT_mm, 2 * b + 2)
                a.activation(onT[:, 1], hd.turned[0], ACT.Copy).then_inc(oT_rdy, 1)
                count = 2 * b + (3 if more else 2)
                turned(count, G1, env.n2T[:, b], g2, b2)
                router_exp(count, 8)
            passes(a, body, B)

        @block.tensor
        def _(pe):
            def turn(count, bank):
                pe.wait_ge(nn_rdy, count)
                transpose4(pe, bank, nn, env.ident[:]).then_inc(nT_mm, 1)

            def logits(count, n, rw):
                pe.wait_ge(sb_rdy, count)
                for k in range(C):
                    last = pe.matmul(G2[:, 0, 0:n], sbr[:, k], rw[:, k], start=(k == 0), stop=(k == C - 1))
                last.then_inc(lg_mm, 1)

            def project(m):
                product(pe, lambda o: G0[:, o], lambda k, o: wq[:, m, k, chunk(o)],
                        lambda k: n1T[:, k]).then_inc(q_mm, 1)
                product(pe, lambda o: G1[:, o], lambda k, o: wk[:, m, k, chunk(o)],
                        lambda k: n1T[:, k]).then_inc(k_mm, 1)

            def project_v(m):
                product(pe, lambda o: G2[:, o], lambda k, o: n1T[:, k, chunk(o)],
                        lambda k: wv[:, m, k]).then_inc(v_mm, 1)

            turn(1, G0)
            pe.wait_ge(w_in, 16 * loads)
            logits(1, 2, rw1)

            def body(b, more):
                pe.wait_ge(s_rdy, 2 * b + 1)
                project(0)
                pe.wait_ge(z_rdy, 2 * b + 1)
                project_v(0)
                pe.wait_ge(k_rdy, 2 * b + 1)
                pe.wait_ge(v_rdy, 2 * b + 1)
                hd.tensor(pe, 2 * b, {}, lambda: None)
                project(1)
                project_v(1)
                pe.wait_ge(on_rdy, 2 * b + 1)
                transpose4(pe, hd.turned[0], hd.on, env.ident[:]).then_inc(oT_mm, 1)
                pe.wait_ge(k_rdy, 2 * b + 2)
                pe.wait_ge(v_rdy, 2 * b + 2)
                mid = {12: lambda: turn(2 * b + 2, G0), 15: lambda: logits(2 * b + 2, 2, rw1)} if more else {}
                hd.tensor(pe, 2 * b + 1, mid, lambda: pe.wait_ge(oT_rdy, 2 * b + 1))
                pe.wait_ge(on_rdy, 2 * b + 2)
                transpose4(pe, hd.turned[0], hd.on, env.ident[:]).then_inc(oT_mm, 1)
                pe.wait_ge(oT_rdy, 2 * b + 2)
                if more:
                    pe.wait_ge(s_rdy, 2 * b + 2)
                for tc in range(C):
                    for m in range(2):
                        for k in range(C):
                            last = pe.matmul(G0[:, tc], onT[:, m, k, chunk(tc)], wo[:, m, k],
                                             start=(m == 0 and k == 0), stop=(m == 1 and k == C - 1))
                last.then_inc(mh_mm, 1)
                count = 2 * b + (3 if more else 2)
                turn(count, G1)
                logits(count, 8, rw2)
            passes(pe, body, B)


def layer0_experts(nc, env, w, sem_):
    F = 512
    FC = F // P
    J = 4
    with ExitStack() as ctx:
        sb = lambda n, s, d=F32: ctx.enter_context(nc.sbuf_tensor("E0" + n, s, d))
        w1, w2 = sb("w1", [P, J, C, F]), sb("w2", [P, J, FC, D])
        hT = sb("hT", [P, 2, FC, S])
        w_in = [sem_(f"e0_w_in{j}") for j in range(J)]
        h_mm, h_rdy, y_mm, y_used = (sem_("e0_" + n) for n in ("h_mm", "h_rdy", "y_mm", "y_used"))
        block = ctx.enter_context(nc.Block())

        @block.sync
        def _(sp):
            def body(i, more):
                for j in range(J):
                    e = sp.value_load(env.pick[0:1, 2 * i + j // 2, j % 2:j % 2 + 1], min_val=0, max_val=7)
                    if not isinstance(i, int):
                        sp.wait_ge(y_mm, J * i + j - J + 1)
                    sp.dma_start(w1[:, j], w["L0_ffn_fw1"][bass.ds(e, 1)].rearrange("e (k p) f -> p (e k) f", p=P))\
                        .then_inc(w_in[j], 16)
                    sp.dma_start(w2[:, j], w["L0_ffn_fw2"][bass.ds(e, 1)].rearrange("e (k p) f -> p (e k) f", p=P))\
                        .then_inc(w_in[j], 16)
            body(0, True)
            with sp.Fori(1, NI) as i:
                body(i, True)

        @block.tensor
        def _(pe):
            def hidden(i, j):
                pe.wait_ge(w_in[j], 32 * i + 32)
                for half in range(2):
                    for m in range(C):
                        f = C * half + m
                        for k in range(C):
                            last = pe.matmul(env.bank(4 * (j % 2) + half)[:, m], w1[:, j, k, chunk(f)],
                                             env.n2T[:, 2 * i + j // 2, k], start=(k == 0), stop=(k == C - 1))
                last.then_inc(h_mm, 1)

            def output(i, j):
                pe.wait_ge(h_rdy, J * i + j + 1)
                for tc in range(C):
                    for k in range(FC):
                        last = pe.matmul(env.bank(4 * (j % 2) + 2)[:, tc], hT[:, j % 2, k, chunk(tc)], w2[:, j, k],
                                         start=(k == 0), stop=(k == FC - 1))
                last.then_inc(y_mm, 1)

            hidden(0, 0)

            def body(i, more):
                for j in range(J):
                    if j + 1 < J:
                        hidden(i, j + 1)
                    elif more:
                        hidden(i + 1, 0)
                    pe.wait_ge(y_used, J * i + j + 1)
                    output(i, j)
            passes(pe, body)

        @block.scalar
        def _(a):
            def body(i, more):
                for j in range(J):
                    a.wait_ge(h_mm, J * i + j + 1)
                    for half in range(2):
                        last = a.activation(hT[:, j % 2, C * half:C * half + C], env.bank(4 * (j % 2) + half), ACT.Gelu)
                    last.then_inc(h_rdy, 1)
            passes(a, body)

        @block.vector
        def _(v):
            v.sem_inc(y_used, 2)

            def body(i, more):
                for j in range(J):
                    b = 2 * i + j // 2
                    v.wait_ge(y_used, J * i + j + 2)
                    v.wait_ge(y_mm, J * i + j + 1)
                    v.scalar_tensor_tensor(env.x[:, b], env.bank(4 * (j % 2) + 2), env.pick_w[:, b, j % 2:j % 2 + 1],
                                           env.x[:, b], ALU.mult, ALU.add).then_inc(y_used, 1)
            passes(v, body)


class Front:

    def __init__(self, nc, env, ctx, sem_, tag, banks):
        sb = lambda n, s, d=F32: ctx.enter_context(nc.sbuf_tensor(tag + n, s, d))
        self.env, self.banks = env, banks
        self.xn, self.xnT = sb("xn", [P, 2, C, D]), sb("xnT", [P, 2, C, S])
        self.st, self.mv, self.rstd = sb("st", [P, 2, C, 6]), sb("mv", [P, 2, C, 2]), sb("rstd", [P, 2, C])
        (self.st_rdy, self.rstd_rdy, self.xn_rdy, self.xnT_mm, self.xnT_rdy, self.v_ch, self.g_ch) = (
            sem_(tag + n) for n in ("st_rdy", "rstd_rdy", "xn_rdy", "xnT_mm", "xnT_rdy", "fv_ch", "fg_ch"))

    def gpsimd(self, g, i):
        ch = Chain(g, self.g_ch)
        ch.start(2 * i)
        for u in (0, 1):
            g.wait_ge(self.st_rdy, nth(i, u))
            ln_rstd(g, ch, self.mv[:, u], self.rstd[:, u], self.env.mhalf, self.env.eps5).then_inc(self.rstd_rdy, 1)

    def vector(self, v, i):
        ch = Chain(v, self.v_ch)
        ch.start(2 * i)
        for u in (0, 1):
            ln_stats(v, ch, self.env.x[:, 2 * i + u], self.st[:, u], self.mv[:, u], self.env.scrap)\
                .then_inc(self.st_rdy, 1)
        for u in (0, 1):
            v.wait_ge(self.rstd_rdy, nth(i, u))
            ln_apply(v, self.xn[:, u], self.env.x[:, 2 * i + u], self.mv[:, u], self.rstd[:, u])\
                .then_inc(self.xn_rdy, 1)

    def tensor(self, pe, i):
        for u in (0, 1):
            pe.wait_ge(self.xn_rdy, nth(i, u))
            transpose4(pe, self.banks[u], self.xn[:, u], self.env.ident[:]).then_inc(self.xnT_mm, 1)

    def scalar(self, a, i):
        for u in (0, 1):
            a.wait_ge(self.xnT_mm, nth(i, u))
            a.activation(self.xnT[:, u], self.banks[u], ACT.Copy).then_inc(self.xnT_rdy, 1)


def layer1_attention(nc, env, w, sem_):
    TOP = 5
    BIG = 3e38
    with ExitStack() as ctx:
        sb = lambda n, s, d=F32: ctx.enter_context(nc.sbuf_tensor("A1" + n, s, d))
        wq, wk, wv, wo, dft_f, dft_g = (sb(n, [P, C, D]) for n in ("wq", "wk", "wv", "wo", "f", "g"))
        rot, own, inner = sb("rot", [P, KD, KD]), sb("own", [P, 8]), sb("inner", [P, 2])
        fx, fc, fq, fk, sp_, ctx_in, cw, vw = (sb(n, [P, C, D]) for n in
                                               ("fx", "fc", "fq", "fk", "sp", "ctx_in", "cw", "vw"))
        xn = sb("xn", [P, C, D])
        ta, tb, tc_ = (sb(n, [P, C, S]) for n in ("ta", "tb", "tc"))
        corr, rep = sb("corr", [P, C, S + 8]), sb("rep", [P, C, S + 8])
        ex, top, nmax = sb("ex", [P, C, S]), sb("top", [P, C, 8]), sb("nmax", [P, C])
        es, fold, mixr, mix = sb("es", [P, C]), sb("fold", [P, C, KD]), sb("mixr", [P, KD, KD]), sb("mix", [P, C, KD])
        blk = sb("blk", [P, C, P])
        mixT = sb("mixT", [P, C, KD, H])
        st, mv, rstd = sb("st", [P, C, 6]), sb("mv", [P, C, 2]), sb("rstd", [P, C])
        (w_in, c_in, st_rdy, rstd_rdy, xn_rdy, fx_mm, fx_rdy, fc_mm, fc_rdy, fq_mm, fq_rdy, fk_mm, fk_rdy, sp_rdy,
         co_mm, co_rdy, mx_rdy, ex_rdy, blk_rdy, blkT_mm, mixT_rdy, cw_mm, cw_rdy, vw_mm, vw_rdy, o_mm, v_ch, g_ch) = (
            sem_("a1_" + n) for n in (
                "w_in", "c_in", "st_rdy", "rstd_rdy", "xn_rdy", "fx_mm", "fx_rdy", "fc_mm", "fc_rdy", "fq_mm",
                "fq_rdy", "fk_mm", "fk_rdy", "sp_rdy", "co_mm", "co_rdy", "mx_rdy", "ex_rdy", "blk_rdy",
                "blkT_mm", "mixT_rdy", "cw_mm", "cw_rdy", "vw_mm", "vw_rdy", "o_mm", "v_ch", "g_ch"))
        bank = env.bank
        loads = 9
        block = ctx.enter_context(nc.Block())

        @block.sync
        def _(sp):
            for t, n in ((dft_f, "dft_f"), (dft_g, "dft_g"), (wq, "L1_xattn_wq"), (wk, "L1_xattn_wk"),
                         (wv, "L1_xattn_wv"), (wo, "L1_xattn_wo")):
                load_weight(sp, t[:], w[n], w_in)
            sp.dma_start(rot[:], w["rot"]).then_inc(w_in, 16)
            sp.dma_start(own[:], w["own"]).then_inc(w_in, 16)
            sp.dma_start(inner[:], w["inner"]).then_inc(w_in, 16)
            cv = w["ctx_1024"].rearrange("b (c p) d -> b p c d", p=P)
            sp.dma_start(ctx_in[:], cv[0]).then_inc(c_in, 16)
            with sp.Fori(1, B) as b:
                sp.wait_ge(cw_mm, b)
                sp.dma_start(ctx_in[:], cv[bass.ds(b, 1)].rearrange("b p c d -> p (b c) d")).then_inc(c_in, 16)

        @block.gpsimd
        def _(g):
            ch = Chain(g, g_ch)
            with g.Fori(0, B) as b:
                ch.start(b)
                g.wait_ge(st_rdy, b + 1)
                ln_rstd(g, ch, mv, rstd, env.mhalf, env.eps5).then_inc(rstd_rdy, 1)

        @block.vector
        def _(v):
            ch = Chain(v, v_ch)

            def front(b):
                ln_stats(v, ch, env.x[:, b], st, mv, env.scrap).then_inc(st_rdy, 1)
                v.wait_ge(rstd_rdy, b + 1)
                ln_apply(v, xn, env.x[:, b], mv, rstd).then_inc(xn_rdy, 1)

            for t in (corr, rep):
                v.memset(t[:], -BIG)
            v.memset(mixT[:], 0.0)
            v.wait_ge(w_in, 16 * loads)
            ch.start(0)
            front(0)

            def body(b, more):
                ch.start(24 * b + 1)
                v.wait_ge(fc_mm, b + 1)
                v.tensor_copy(fc[:], bank(1)).then_inc(fc_rdy, 1)
                v.wait_ge(cw_mm, b + 1)
                v.tensor_copy(cw[:], bank(5)).then_inc(cw_rdy, 1)
                v.wait_ge(fk_mm, b + 1)
                ch.link(v.tensor_copy(fk[:], bank(3)))
                v.wait_ge(fq_rdy, b + 1)
                v.tensor_tensor(ta[:], fq[:], fk[:], ALU.mult)
                v.tensor_tensor(tb[:, 0], fq[:, 1], fk[:, 0], ALU.mult)
                ch.link(v.tensor_tensor(tb[:, 1], fq[:, 0], fk[:, 1], ALU.mult))
                v.scalar_tensor_tensor(sp_[:, 0], ta[:, 1], inner[:, 0:1], ta[:, 0], ALU.mult, ALU.add)
                v.tensor_scalar(tc_[:, 1], ta[:, 1], inner[:, 1:2], None, ALU.mult)
                ch.link(v.tensor_tensor(tc_[:, 0], tb[:, 0], tb[:, 1], ALU.subtract))
                v.scalar_tensor_tensor(sp_[:, 1], tc_[:, 0], inner[:, 0:1], tc_[:, 1], ALU.mult, ALU.add)\
                    .then_inc(sp_rdy, 1)
                if more:
                    front(b + 1)
                v.wait_ge(co_mm, b + 1)
                ch.link(v.tensor_copy(corr[:, :, 0:S], bank(4)))
                for c in range(C):
                    v.memset(env.scrap[:], 0.0)
                    ch.link(v.max(top[:, c], corr[:, c, 0:S]))
                    v.tensor_scalar(nmax[:, c:c + 1], top[:, c, 0:1], -1.0, None, ALU.mult).then_inc(mx_rdy, 1)
                    ch.link(v.memset(top[:, c, TOP:8], -BIG))
                    v.memset(env.scrap[:], 0.0)
                    ch.link(v.match_replace(rep[:, c], top[:, c], corr[:, c], BIG))
                    v.wait_ge(ex_rdy, 2 * b + c + 1)
                    ch.link(v.scalar_tensor_tensor(ex[:, c], rep[:, c, 0:S], BIG, ex[:, c], ALU.is_ge, ALU.mult,
                                                   accum_out=es[:, c:c + 1]))
                    ch.link(v.reciprocal(es[:, c:c + 1], es[:, c:c + 1]))
                    ch.link(v.tensor_reduce(fold[:, c], ex[:, c].rearrange("p (m r) -> p r m", r=KD), AX.X, ALU.add))
                    ch.link(v.tensor_scalar(fold[:, c], fold[:, c], es[:, c:c + 1], None, ALU.mult))
                    ch.link(v.tensor_tensor(mixr[:], rot[:], fold[:, c].unsqueeze(1).broadcast_to([P, KD, KD]), ALU.mult))
                    ch.link(v.tensor_reduce(mix[:, c], mixr[:], AX.X, ALU.add))
                    last = v.tensor_tensor(blk[:, c].rearrange("p (h k) -> p h k", k=KD),
                                           own[:].unsqueeze(2).broadcast_to([P, 8, KD]),
                                           mix[:, c].unsqueeze(1).broadcast_to([P, 8, KD]), ALU.mult)
                last.then_inc(blk_rdy, 1)
                v.wait_ge(blkT_mm, b + 1)
                for c in range(C):
                    last = v.tensor_copy(mixT[:, c, :, 8 * c:8 * c + 8],
                                         bank(5)[:, c, 0:P].rearrange("p (h k) -> p k h", k=KD))
                last.then_inc(mixT_rdy, 1)
                v.wait_ge(o_mm, b + 1)
                ch.link(v.scalar_tensor_tensor(env.x[:, b], bank(7), env.tg[:, 1:2], env.x[:, b], ALU.mult, ALU.add))
                if more:
                    ch.end(24)
            passes(v, body, B)

        @block.scalar
        def _(a):
            def body(b, more):
                a.wait_ge(fx_mm, b + 1)
                a.activation(fx[:], bank(0), ACT.Copy).then_inc(fx_rdy, 1)
                a.wait_ge(fq_mm, b + 1)
                a.activation(fq[:], bank(2), ACT.Copy).then_inc(fq_rdy, 1)
                a.wait_ge(vw_mm, b + 1)
                a.activation(vw[:], bank(6), ACT.Copy).then_inc(vw_rdy, 1)
                for c in range(C):
                    a.wait_ge(mx_rdy, 2 * b + c + 1)
                    a.activation(ex[:, c], corr[:, c, 0:S], ACT.Exp, bias=nmax[:, c:c + 1]).then_inc(ex_rdy, 1)
            passes(a, body, B)

        @block.tensor
        def _(pe):
            pe.wait_ge(w_in, 16 * loads)

            def transforms(b):
                pe.wait_ge(xn_rdy, b + 1)
                product(pe, lambda m: bank(0)[:, m], lambda k, m: xn[:, k, chunk(m)],
                        lambda k: dft_f[:, k]).then_inc(fx_mm, 1)
                pe.wait_ge(c_in, 16 * b + 16)
                product(pe, lambda m: bank(1)[:, m], lambda k, m: ctx_in[:, k, chunk(m)],
                        lambda k: dft_f[:, k]).then_inc(fc_mm, 1)
                product(pe, lambda m: bank(5)[:, m], lambda k, m: ctx_in[:, k, chunk(m)],
                        lambda k: wo[:, k]).then_inc(cw_mm, 1)

            transforms(0)

            def body(b, more):
                pe.wait_ge(fx_rdy, b + 1)
                product(pe, lambda m: bank(2)[:, m], lambda k, m: fx[:, k, chunk(m)],
                        lambda k: wq[:, k]).then_inc(fq_mm, 1)
                pe.wait_ge(fc_rdy, b + 1)
                product(pe, lambda m: bank(3)[:, m], lambda k, m: fc[:, k, chunk(m)],
                        lambda k: wk[:, k]).then_inc(fk_mm, 1)
                pe.wait_ge(cw_rdy, b + 1)
                product(pe, lambda m: bank(6)[:, m], lambda k, m: wv[:, k, chunk(m)],
                        lambda k: cw[:, k]).then_inc(vw_mm, 1)
                pe.wait_ge(sp_rdy, b + 1)
                product(pe, lambda m: bank(4)[:, m], lambda k, m: sp_[:, k, chunk(m)],
                        lambda k: dft_g[:, k]).then_inc(co_mm, 1)
                pe.wait_ge(blk_rdy, b + 1)
                for c in range(C):
                    last = pe.transpose(bank(5)[:, c, 0:P], blk[:, c], env.ident[:])
                last.then_inc(blkT_mm, 1)
                pe.wait_ge(mixT_rdy, b + 1)
                if more:
                    transforms(b + 1)
                pe.wait_ge(vw_rdy, b + 1)
                for tc in range(C):
                    for k in range(C):
                        last = pe.matmul(bank(7)[:, tc], mixT[:, k, 8 * tc:8 * tc + 8], vw[:, k],
                                         start=(k == 0), stop=(k == C - 1))
                last.then_inc(o_mm, 1)
            passes(pe, body, B)


def first_of(v, ch, sel, val, first, gt, eq, n, count):
    shape = [P, C, n, n]
    other = val.unsqueeze(2).broadcast_to(shape)
    this = val.unsqueeze(3).broadcast_to(shape)
    ahead = first.unsqueeze(1).broadcast_to([P, C, n, n])
    for c in range(C):
        v.tensor_tensor(gt[:, c], other[:, c], this[:, c], ALU.is_gt)
        last = v.tensor_tensor(eq[:, c], other[:, c], this[:, c], ALU.is_equal)
    ch.link(last)
    for c in range(C):
        last = v.tensor_tensor(eq[:, c], eq[:, c], ahead[:, c], ALU.mult)
    ch.link(last)
    ch.link(v.tensor_tensor(gt, gt, eq, ALU.add))
    ch.link(v.tensor_reduce(sel, gt, AX.X, ALU.add))
    return v.tensor_scalar(sel, sel, float(count), None, ALU.is_lt)


def layer1_experts(nc, env, w, sem_):
    E, I = 8, 128
    EX = E + 2
    with ExitStack() as ctx:
        sb = lambda n, s, d=F32: ctx.enter_context(nc.sbuf_tensor("E1" + n, s, d))
        bank = env.bank
        fr = Front(nc, env, ctx, sem_, "e1", [bank(6), bank(6)])
        wg, wu = sb("wg", [P, EX, C, I]), sb("wu", [P, EX, C, I])
        wd = sb("wd", [P, EX, D])
        gw, gb, first = sb("gw", [P, C, E]), sb("gb", [P, E]), sb("first", [P, E, E])
        sfc, tmp, sel = (sb(n, [P, C, E]) for n in ("sfc", "tmp", "sel"))
        score2 = sb("score", [P, 2, C, E])
        gs, gsel = sb("gs", [P, C, 4]), sb("gsel", [P, C, 4])
        gt, eq, gt4, eq4 = sb("gt", [P, C, E, E]), sb("eq", [P, C, E, E]), sb("gt4", [P, C, 4, 4]), sb("eq4", [P, C, 4, 4])
        ws = sb("ws", [P, C])
        wt = sb("wt", [P, 2, C, EX])
        sg, hT = sb("sg", [P, 2, S]), sb("hT", [P, 2, S])
        (w_in, lg_mm, sc_rdy, wt_rdy, gu_mm, sg_rdy, h_rdy, y_mm, y_used, v_ch) = (
            sem_("e1_" + n) for n in ("w_in", "lg_mm", "sc_rdy", "wt_rdy", "gu_mm", "sg_rdy", "h_rdy", "y_mm",
                                      "y_used", "v_ch"))
        loads = 13
        block = ctx.enter_context(nc.Block())

        @block.sync
        def _(sp):
            for t, n in ((wg, "w_gate"), (wu, "w_up")):
                for k in range(C):
                    sp.dma_start(t[:, 0:E, k], w["L1_ffn_" + n].rearrange("e (k p) i -> k p e i", p=P)[k])\
                        .then_inc(w_in, 16)
            for t, n in ((wg, "sw_gate"), (wu, "sw_up")):
                for j in range(2):
                    sp.dma_start(t[:, E + j], w["L1_ffn_" + n].rearrange("(k p) n -> p k n", p=P)[:, :, j * I:(j + 1) * I])\
                        .then_inc(w_in, 16)
            sp.dma_start(wd[:, 0:E], w["L1_ffn_w_down"].rearrange("e i n -> i e n")).then_inc(w_in, 16)
            sp.dma_start(wd[:, E:EX], w["L1_ffn_sw_down"].rearrange("(e i) n -> i e n", i=I)).then_inc(w_in, 16)
            sp.dma_start(gw[:], w["L1_ffn_gate_w"].rearrange("(k p) n -> p k n", p=P)).then_inc(w_in, 16)
            sp.dma_start(gb[:], rows(w["L1_ffn_gate_bias"])).then_inc(w_in, 16)
            sp.dma_start(first[:], w["first"]).then_inc(w_in, 16)

        @block.gpsimd
        def _(g):
            fr.gpsimd(g, 0)

            def body(i, more):
                if more:
                    fr.gpsimd(g, i + 1)
            passes(g, body)

        @block.vector
        def _(v):
            ch = Chain(v, v_ch)
            fr.vector(v, 0)
            v.wait_ge(w_in, 16 * loads)

            def gate(i, u):
                v.wait_ge(sc_rdy, nth(i, u))
                score = score2[:, u]
                ch.link(v.tensor_scalar(score, score, 1.0, None, ALU.add))
                ch.link(v.reciprocal(score, score))
                for c in range(C):
                    last = v.tensor_tensor(sfc[:, c], score[:, c], gb[:], ALU.add)
                ch.link(last)
                pairs = sfc[:].rearrange("p c (g t) -> p c g t", t=2)
                ch.link(v.tensor_tensor(gs[:], pairs[:, :, :, 0], pairs[:, :, :, 1], ALU.add))
                ch.link(first_of(v, ch, gsel[:], gs[:], first[:, 0:4, 0:4], gt4[:], eq4[:], 4, 2))
                ch.link(v.tensor_tensor(tmp[:].rearrange("p c (g t) -> p (c g) t", t=2),
                                        sfc[:].rearrange("p c (g t) -> p (c g) t", t=2),
                                        gsel[:].rearrange("p c g -> p (c g)").unsqueeze(2).broadcast_to([P, C * 4, 2]),
                                        ALU.mult))
                ch.link(first_of(v, ch, sel[:], tmp[:], first[:], gt[:], eq[:], E, 2))
                ch.link(v.tensor_tensor(sel[:], sel[:], sfc[:], ALU.mult))
                ch.link(v.tensor_reduce(ws[:], sel[:], AX.X, ALU.add))
                ch.link(v.tensor_scalar(ws[:], ws[:], 1e-20, None, ALU.add))
                ch.link(v.reciprocal(ws[:], ws[:]))
                ch.link(v.tensor_scalar(ws[:], ws[:], 2.5, env.tg[:, 5:6], ALU.mult, ALU.mult))
                for c in range(C):
                    v.tensor_scalar(wt[:, u, c, 0:E], sel[:, c], ws[:, c:c + 1], None, ALU.mult)
                    last = v.tensor_scalar(wt[:, u, c, E:EX], first[:, 0, 0:2], 0.0, env.tg[:, 5:6], ALU.mult, ALU.add)
                ch.link(last)

            def body(i, more):
                ch.start((2 * 21 + 2 * EX) * i)
                for u in (0, 1):
                    gate(i, u)
                for e in range(EX):
                    for u in (0, 1):
                        n = 2 * EX * i + 2 * e + u + 1
                        b = 2 * i + u
                        v.wait_ge(sg_rdy, n)
                        v.tensor_tensor(hT[:, u], bank(u)[:, 1], sg[:, u], ALU.mult).then_inc(h_rdy, 1)
                        v.wait_ge(y_mm, n)
                        for c in range(C):
                            last = v.scalar_tensor_tensor(env.x[:, b, c], bank(2 + u)[:, c], wt[:, u, c, e:e + 1],
                                                          env.x[:, b, c], ALU.mult, ALU.add)
                        ch.link(last)
                    if e == EX - 3 and more:
                        fr.vector(v, i + 1)
                ch.end(2 * 21 + 2 * EX)
            passes(v, body)

        @block.scalar
        def _(a):
            fr.scalar(a, 0)

            def body(i, more):
                for u in (0, 1):
                    a.wait_ge(lg_mm, nth(i, u))
                    a.activation(score2[:, u], bank(7)[:, :, 0:E], ACT.Exp, scale=-1.0).then_inc(sc_rdy, 1)
                for e in range(EX):
                    for u in (0, 1):
                        a.wait_ge(gu_mm, 2 * EX * i + 2 * e + u + 1)
                        a.activation(sg[:, u], bank(u)[:, 0], ACT.Silu).then_inc(sg_rdy, 1)
                if more:
                    fr.scalar(a, i + 1)
            passes(a, body)

        @block.tensor
        def _(pe):
            def front(i):
                for u in (0, 1):
                    pe.wait_ge(fr.xn_rdy, nth(i, u))
                    if u == 1:
                        pe.wait_ge(fr.xnT_rdy, nth(i, 0))
                    transpose4(pe, bank(6), fr.xn[:, u], env.ident[:]).then_inc(fr.xnT_mm, 1)

            front(0)
            pe.wait_ge(w_in, 16 * loads)

            def up(i, e, u):
                if e >= 1:
                    pe.wait_ge(h_rdy, 2 * EX * i + 2 * (e - 1) + u + 1)
                for half, wt_ in ((0, wg), (1, wu)):
                    for k in range(C):
                        last = pe.matmul(bank(u)[:, half], wt_[:, e, k], fr.xnT[:, u, k], start=(k == 0), stop=(k == C - 1))
                last.then_inc(gu_mm, 1)

            def body(i, more):
                for u in (0, 1):
                    pe.wait_ge(fr.xnT_rdy, nth(i, u))
                    if u == 1:
                        pe.wait_ge(sc_rdy, nth(i, 0))
                    for tc in range(C):
                        for k in range(C):
                            last = pe.matmul(bank(7)[:, tc, 0:E], fr.xnT[:, u, k, chunk(tc)], gw[:, k],
                                             start=(k == 0), stop=(k == C - 1))
                    last.then_inc(lg_mm, 1)
                up(i, 0, 0)
                up(i, 0, 1)
                for e in range(EX):
                    for u in (0, 1):
                        pe.wait_ge(h_rdy, 2 * EX * i + 2 * e + u + 1)
                        if e >= 1:
                            pe.wait_ge(v_ch, (2 * 21 + 2 * EX) * i + 2 * 21 + 2 * (e - 1) + u + 1)
                        for tc in range(C):
                            last = pe.matmul(bank(2 + u)[:, tc], hT[:, u, chunk(tc)], wd[:, e], start=True, stop=True)
                        last.then_inc(y_mm, 1)
                        if e + 1 < EX:
                            up(i, e + 1, u)
                if more:
                    front(i + 1)
            passes(pe, body)


def layer2_attention(nc, env, w, sem_):
    LOW = -2.0 ** 126
    with ExitStack() as ctx:
        sb = lambda n, s, d=F32: ctx.enter_context(nc.sbuf_tensor("A2" + n, s, d))
        hd = Heads(nc, env, ctx, sem_, "a2", masked=True)
        wq, wk, wv, wp = (sb(n, [P, C, D]) for n in ("wq", "wk", "wv", "wp"))
        bp = sb("bp", [P, D])
        flags = sb("flags", [1, B, S], I32)
        low, one_row = sb("low", [P, B, S], BF16), sb("one_row", [P, P], BF16)
        xn, xnT, cT, onT, y = (sb(n, [P, C, D]) for n in ("xn", "xnT", "cT", "onT", "y"))
        st, mv, rstd = sb("st", [P, C, 6]), sb("mv", [P, C, 2]), sb("rstd", [P, C])
        (w_in, zeroed, low_rdy, st_rdy, rstd_rdy, xn_rdy, xnT_mm, xnT_rdy, cT_rdy, q_mm, k_mm, v_mm, k_rdy, v_rdy,
         on_rdy, oT_mm, oT_rdy, y_mm, y_used, v_ch, g_ch) = (
            sem_("a2_" + n) for n in (
                "w_in", "zeroed", "low_rdy", "st_rdy", "rstd_rdy", "xn_rdy", "xnT_mm", "xnT_rdy", "cT_rdy", "q_mm",
                "k_mm", "v_mm", "k_rdy", "v_rdy", "on_rdy", "oT_mm", "oT_rdy", "y_mm", "y_used", "v_ch",
                "g_ch"))
        G0, G1, G2 = env.bank(5), env.bank(6), env.bank(7)
        loads = 7
        block = ctx.enter_context(nc.Block())

        @block.sync
        def _(sp):
            load_weight(sp, wq[:], w["L2_xattn_Wq"], w_in)
            load_weight(sp, wk[:], w["L2_xattn_Wkv"][:, 0:D], w_in)
            load_weight(sp, wv[:], w["L2_xattn_Wkv"][:, D:2 * D], w_in)
            load_weight(sp, wp[:], w["L2_xattn_Wproj"], w_in)
            sp.dma_start(bp[:], rows(w["L2_xattn_bproj"])).then_inc(w_in, 16)
            sp.dma_start(hd.own[:], w["own"]).then_inc(w_in, 16)
            sp.dma_start(flags[:], w["mask_BxS2_bk0"].rearrange("(a b) s -> a b s", a=1)).then_inc(w_in, 16)

        @block.gpsimd
        def _(g):
            ch = Chain(g, g_ch)
            g.memset(low[:], 0.0).then_inc(zeroed, 1)
            g.memset(one_row[:], 0.0).then_inc(zeroed, 1)

            def front(b):
                ch.start(b)
                g.wait_ge(st_rdy, b + 1)
                ln_rstd(g, ch, mv, rstd, env.mhalf, env.eps5).then_inc(rstd_rdy, 1)

            def copy_ctx(b):
                g.tensor_copy(cT[:], env.ctxT[:, b]).then_inc(cT_rdy, 1)

            front(0)
            copy_ctx(0)

            def body(b, more):
                if more:
                    front(b + 1)
                    g.wait_ge(v_mm, b + 1)
                    g.tensor_tensor(rstd_scrap[:], env.eps5[:], env.eps5[:], ALU.add)
                    copy_ctx(b + 1)
            rstd_scrap = sb("rscrap", [P, C])
            passes(g, body, B)

        @block.vector
        def _(v):
            ch = Chain(v, v_ch)
            v.sem_inc(y_used, 1)

            def front_a(b):
                ln_stats(v, ch, env.x[:, b], st, mv, env.scrap).then_inc(st_rdy, 1)

            def front_b(b):
                v.wait_ge(rstd_rdy, b + 1)
                ln_apply(v, xn, env.x[:, b], mv, rstd).then_inc(xn_rdy, 1)

            v.wait_ge(zeroed, 2)
            v.memset(one_row[0:1, :], 1.0).then_inc(low_rdy, 1)
            v.wait_ge(w_in, 16 * loads)
            v.tensor_scalar(low[0:1], flags[:], 0, LOW, ALU.not_equal, ALU.mult).then_inc(low_rdy, 1)
            ch.start(0)
            front_a(0)
            front_b(0)

            def body(b, more):
                ch.start(4 * b + 1)
                v.wait_ge(q_mm, b + 1)
                ch.link(v.tensor_scalar(hd.qT[:], G0, KD ** -0.5, None, ALU.mult))
                v.wait_ge(v_mm, b + 1)
                v.tensor_copy(hd.vt[:], G2).then_inc(v_rdy, 1)
                hd.vector(v, b, {5: lambda: front_a(b + 1), 8: lambda: front_b(b + 1)} if more else {})
                hd.normalise(v, ch, b).then_inc(on_rdy, 1)
                v.wait_ge(y_mm, b + 1)
                for c in range(C):
                    last = v.tensor_tensor(y[:, c], G0[:, c], bp[:], ALU.add)
                last.then_inc(y_used, 1)
                v.wait_ge(y_used, b + 2)
                last = v.scalar_tensor_tensor(env.x[:, b], y[:], env.tg[:, 2:3], env.x[:, b], ALU.mult, ALU.add)
                ch.link(last)
                if more:
                    ch.end(4)
            passes(v, body, B)

        @block.scalar
        def _(a):
            def front(b):
                a.wait_ge(xnT_mm, b + 1)
                a.activation(xnT[:], G1, ACT.Copy).then_inc(xnT_rdy, 1)

            front(0)

            def body(b, more):
                a.wait_ge(k_mm, b + 1)
                a.activation(hd.kT[:], G1, ACT.Copy).then_inc(k_rdy, 1)
                hd.scalar(a, b, {12: lambda: front(b + 1)} if more else {})
                a.wait_ge(oT_mm, b + 1)
                a.activation(onT[:], hd.turned[0], ACT.Copy).then_inc(oT_rdy, 1)
            passes(a, body, B)

        @block.tensor
        def _(pe):
            def front(b):
                pe.wait_ge(xn_rdy, b + 1)
                transpose4(pe, G1, xn, env.ident[:]).then_inc(xnT_mm, 1)

            front(0)
            pe.wait_ge(w_in, 16 * loads)
            pe.wait_ge(low_rdy, 2)

            def body(b, more):
                pe.wait_ge(xnT_rdy, b + 1)
                pe.wait_ge(y_used, b + 1)
                product(pe, lambda m: G0[:, m], lambda k, m: wq[:, k, chunk(m)], lambda k: xnT[:, k]).then_inc(q_mm, 1)
                pe.wait_ge(cT_rdy, b + 1)
                product(pe, lambda m: G1[:, m], lambda k, m: wk[:, k, chunk(m)], lambda k: cT[:, k]).then_inc(k_mm, 1)
                product(pe, lambda m: G2[:, m], lambda k, m: cT[:, k, chunk(m)], lambda k: wv[:, k]).then_inc(v_mm, 1)
                pe.wait_ge(k_rdy, b + 1)
                pe.wait_ge(v_rdy, b + 1)

                def mask(bank):
                    pe.matmul(bank, one_row[:], low[:, b].unsqueeze(1).broadcast_to([P, C, S]),
                              start=True, stop=False, skip_group_check=True)
                hd.tensor(pe, b, {10: lambda: front(b + 1)} if more else {}, lambda: None, mask)
                pe.wait_ge(on_rdy, b + 1)
                transpose4(pe, hd.turned[0], hd.on, env.ident[:]).then_inc(oT_mm, 1)
                pe.wait_ge(oT_rdy, b + 1)
                product(pe, lambda m: G0[:, m], lambda k, m: onT[:, k, chunk(m)], lambda k: wp[:, k]).then_inc(y_mm, 1)
            passes(pe, body, B)


def layer2_experts(nc, env, w, sem_):
    E, F = 8, 1024
    FC = F // P
    with ExitStack() as ctx:
        sb = lambda n, s, d=F32: ctx.enter_context(nc.sbuf_tensor("E2" + n, s, d))
        w1, w2 = sb("w1", [P, 2, C, F]), sb("w2", [P, 2, FC, D])
        b1, b2 = sb("b1", [P, 2, FC]), sb("b2", [P, 2, C])
        wa, wn, ba, bn = sb("wa", [P, C, D]), sb("wn", [P, C, D]), sb("ba", [P, C]), sb("bn", [P, D])
        gain, bias = sb("gain", [P, C]), sb("bias", [P, C])
        xn, nn, n2T, xaT, yT, z = (sb(n, [P, 2, C, D]) for n in ("xn", "nn", "n2T", "xaT", "yT", "z"))
        hT = sb("hT", [P, 2, FC, S])
        st, mv, rstd = sb("st", [P, 2, C, 6]), sb("mv", [P, 2, C, 2]), sb("rstd", [P, 2, C])
        e_in = [sem_(f"e2_in{k}") for k in range(2)]
        (w_in, st_rdy, rstd_rdy, nn_rdy, nT_mm, nT_rdy, xa_mm, xa_rdy, h_mm, h_rdy, y_mm, y_rdy, z_mm, z_rdy, zg_rdy,
         v_ch, f_ch, g_ch) = (
            sem_("e2_" + n) for n in ("w_in", "st_rdy", "rstd_rdy", "nn_rdy", "nT_mm", "nT_rdy", "xa_mm", "xa_rdy",
                                      "h_mm", "h_rdy", "y_mm", "y_rdy", "z_mm", "z_rdy", "zg_rdy", "v_ch", "f_ch",
                                      "g_ch"))
        A, H0, H1, Y = ([env.bank(4 * u + j) for u in (0, 1)] for j in range(4))
        loads = 6
        block = ctx.enter_context(nc.Block())

        def experts(eng, body):
            def two(i, more):
                body(2 * i, True, 0)
                body(2 * i + 1, more, 1)
            passes(eng, two, E // 2)

        @block.sync
        def _(sp):
            load_weight(sp, wa[:], w["L2_ffn_attn_w"], w_in)
            load_weight(sp, wn[:], w["L2_ffn_next_w"], w_in)
            sp.dma_start(ba[:], w["L2_ffn_attn_b"]).then_inc(w_in, 16)
            sp.dma_start(bn[:], rows(w["L2_ffn_next_b"])).then_inc(w_in, 16)
            sp.dma_start(gain[:], w["L2_ffn_ln_g"]).then_inc(w_in, 16)
            sp.dma_start(bias[:], w["L2_ffn_ln_b"]).then_inc(w_in, 16)
            b1v = w["L2_ffn_b1"].rearrange("p (e f) -> e p f", e=E)
            b2v = w["L2_ffn_b2"].rearrange("p (e c) -> e p c", e=E)

            def load(e, k):
                at = bass.ds(e, 1)
                sp.dma_start(w1[:, k], w["L2_ffn_w1"][at].rearrange("e (k p) f -> p (e k) f", p=P)).then_inc(e_in[k], 16)
                sp.dma_start(w2[:, k], w["L2_ffn_w2"][at].rearrange("e (k p) f -> p (e k) f", p=P)).then_inc(e_in[k], 16)
                sp.dma_start(b1[:, k], b1v[at].rearrange("e p f -> p (e f)")).then_inc(e_in[k], 16)
                sp.dma_start(b2[:, k], b2v[at].rearrange("e p f -> p (e f)")).then_inc(e_in[k], 16)

            load(0, 0)
            load(1, 1)
            with sp.Fori(1, E // 2) as i:
                for k in range(2):
                    sp.wait_ge(y_rdy, 4 * i + 2 * k - 2)
                    load(2 * i + k, k)

        @block.gpsimd
        def _(g):
            ch = Chain(g, g_ch)

            def front(e):
                ch.start(4 * e)
                for n in range(4):
                    u = n % 2
                    g.wait_ge(st_rdy, 4 * e + n + 1)
                    ln_rstd(g, ch, mv[:, u], rstd[:, u], env.mhalf, env.eps5).then_inc(rstd_rdy, 1)
            front(0)

            def body(e, more, k):
                if more:
                    front(e + 1)
            experts(g, body)

        @block.vector
        def _(v):
            ch, fch = Chain(v, v_ch), Chain(v, f_ch)

            def front(e):
                fch.start(6 * e)
                for u in (0, 1):
                    ln_stats(v, fch, env.x[:, e + E * u], st[:, u], mv[:, u], env.scrap).then_inc(st_rdy, 1)
                for u in (0, 1):
                    v.wait_ge(rstd_rdy, 4 * e + u + 1)
                    fch.link(ln_apply(v, xn[:, u], env.x[:, e + E * u], mv[:, u], rstd[:, u]))
                    ln_stats(v, fch, xn[:, u], st[:, u], mv[:, u], env.scrap).then_inc(st_rdy, 1)
                for u in (0, 1):
                    v.wait_ge(rstd_rdy, 4 * e + u + 3)
                    ln_apply(v, nn[:, u], xn[:, u], mv[:, u], rstd[:, u]).then_inc(nn_rdy, 1)

            front(0)
            v.wait_ge(w_in, 16 * loads)

            def body(e, more, k):
                for u in (0, 1):
                    if u == 1 and more:
                        front(e + 1)
                    v.wait_ge(y_mm, nth(e, u))
                    for c in range(C):
                        last = v.tensor_scalar(yT[:, u, c], Y[u][:, c], b2[:, k, c:c + 1], None, ALU.add)
                    last.then_inc(y_rdy, 1)
                for u in (0, 1):
                    v.wait_ge(z_mm, nth(e, u))
                    for c in range(C):
                        last = v.tensor_tensor(z[:, u, c], A[u][:, c], bn[:], ALU.add)
                    last.then_inc(z_rdy, 1)
                for u in (0, 1):
                    v.wait_ge(zg_rdy, nth(e, u))
                    b = e + E * u
                    v.scalar_tensor_tensor(env.x[:, b], z[:, u], env.tg[:, 6:7], env.x[:, b], ALU.mult, ALU.add)
            experts(v, body)

        @block.scalar
        def _(a):
            def front(e):
                for u in (0, 1):
                    a.wait_ge(nT_mm, nth(e, u))
                    for c in range(C):
                        last = a.activation(n2T[:, u, c], A[u][:, c], ACT.Identity, scale=gain[:, c:c + 1],
                                            bias=bias[:, c:c + 1])
                    last.then_inc(nT_rdy, 1)

            a.wait_ge(w_in, 16 * loads)
            front(0)

            def body(e, more, k):
                for u in (0, 1):
                    a.wait_ge(xa_mm, nth(e, u))
                    for c in range(C):
                        last = a.activation(xaT[:, u, c], A[u][:, c], ACT.Identity, bias=ba[:, c:c + 1])
                    last.then_inc(xa_rdy, 1)
                for q in range(FC // C):
                    for u in (0, 1):
                        a.wait_ge(h_mm, 8 * e + 2 * q + u + 1)
                        for c in range(C):
                            f = C * q + c
                            last = a.activation(hT[:, u, f], (H0, H1)[q % 2][u][:, c], ACT.Gelu, bias=b1[:, k, f:f + 1])
                        last.then_inc(h_rdy, 1)
                for u in (0, 1):
                    a.wait_ge(z_rdy, nth(e, u))
                    a.activation(z[:, u], z[:, u], ACT.Gelu).then_inc(zg_rdy, 1)
                if more:
                    front(e + 1)
            experts(a, body)

        @block.tensor
        def _(pe):
            def front(e):
                for u in (0, 1):
                    pe.wait_ge(nn_rdy, nth(e, u))
                    if not (isinstance(e, int) and e == 0):
                        pe.wait_ge(z_rdy, nth(e - 1, u))
                    transpose4(pe, A[u], nn[:, u], env.ident[:]).then_inc(nT_mm, 1)

            front(0)
            pe.wait_ge(w_in, 16 * loads)

            def body(e, more, k):
                pe.wait_ge(e_in[k], 32 * (e - k) + 64)
                for u in (0, 1):
                    pe.wait_ge(nT_rdy, nth(e, u))
                    for m in range(C):
                        for kk in range(C):
                            pe.matmul(A[u][:, m], wa[:, kk, chunk(m)], n2T[:, u, kk], start=(kk == 0), stop=False,
                                      skip_group_check=True)
                        for tc in range(C):
                            last = pe.matmul(A[u][:, m, chunk(tc)], xn[:, u, tc, chunk(m)], env.ident[:],
                                             start=False, stop=True, skip_group_check=True)
                    last.then_inc(xa_mm, 1)
                for q in range(FC // C):
                    for u in (0, 1):
                        if q == 0:
                            pe.wait_ge(xa_rdy, nth(e, u))
                        if q >= 2:
                            pe.wait_ge(h_rdy, 8 * e + 2 * (q - 2) + u + 1)
                        for c in range(C):
                            for kk in range(C):
                                last = pe.matmul((H0, H1)[q % 2][u][:, c], w1[:, k, kk, chunk(C * q + c)],
                                                 xaT[:, u, kk], start=(kk == 0), stop=(kk == C - 1))
                        last.then_inc(h_mm, 1)
                for u in (0, 1):
                    pe.wait_ge(h_rdy, 8 * e + 6 + u + 1)
                    product(pe, lambda m: Y[u][:, m], lambda f, m: w2[:, k, f, chunk(m)], lambda f: hT[:, u, f],
                            K=FC).then_inc(y_mm, 1)
                for u in (0, 1):
                    pe.wait_ge(y_rdy, nth(e, u))
                    product(pe, lambda m: A[u][:, m], lambda kk, m: yT[:, u, kk, chunk(m)],
                            lambda kk: wn[:, kk]).then_inc(z_mm, 1)
                if more:
                    front(e + 1)
            experts(pe, body)


def layer3_attention(nc, env, w, sem_):
    with ExitStack() as ctx:
        sb = lambda n, s, d=F32: ctx.enter_context(nc.sbuf_tensor("A3" + n, s, d))
        T0, T1, T2, T3 = ([env.bank(4 * u + j) for u in (0, 1)] for j in range(4))
        fr = Front(nc, env, ctx, sem_, "a3", T0)
        wq, wk, wv, wo = (sb(n, [P, C, D]) for n in ("wq", "wk", "wv", "wo"))
        bqk, bo, bv, own = sb("bqk", [P, 2, D]), sb("bo", [P, D]), sb("bv", [P, C]), sb("own", [P, 8])
        cT, vT, on, onT, y, prod = (sb(n, [P, 2, C, D]) for n in ("cT", "vT", "on", "onT", "y", "prod"))
        qk, ex = sb("qk", [P, 2, 2, C, D]), sb("ex", [P, 2, 2, C, D])
        sm, den = sb("sm", [P, 2, C, P]), sb("den", [P, 2, C, H])
        (w_in, cT_rdy, q_mm, k_mm, v_mm, v_rdy, mn_rdy, ex_rdy, qk_rdy, s_mm, s_rdy, o_mm, on_rdy, oT_mm, oT_rdy,
         y_mm, y_used, v_ch) = (
            sem_("a3_" + n) for n in ("w_in", "cT_rdy", "q_mm", "k_mm", "v_mm", "v_rdy", "mn_rdy", "ex_rdy",
                                      "qk_rdy", "s_mm", "s_rdy", "o_mm", "on_rdy", "oT_mm", "oT_rdy", "y_mm", "y_used",
                                      "v_ch"))
        loads = 9
        block = ctx.enter_context(nc.Block())

        @block.sync
        def _(sp):
            for t, n in ((wq, "Wq"), (wk, "Wk"), (wv, "Wv"), (wo, "Wo")):
                load_weight(sp, t[:], w["L3_xattn_" + n], w_in)
            sp.dma_start(bqk[:, 0], rows(w["L3_xattn_bq"])).then_inc(w_in, 16)
            sp.dma_start(bqk[:, 1], rows(w["L3_xattn_bk"])).then_inc(w_in, 16)
            sp.dma_start(bo[:], rows(w["L3_xattn_bo"])).then_inc(w_in, 16)
            sp.dma_start(bv[:], w["L3_xattn_bv"]).then_inc(w_in, 16)
            sp.dma_start(own[:], w["own"]).then_inc(w_in, 16)

        @block.gpsimd
        def _(g):
            def front(i):
                fr.gpsimd(g, i)
                for u in (0, 1):
                    g.tensor_copy(cT[:, u], env.ctxT[:, 2 * i + u]).then_inc(cT_rdy, 1)
            front(0)

            def body(i, more):
                if more:
                    g.wait_ge(v_mm, nth(i, 1))
                    front(i + 1)
            passes(g, body)

        @block.vector
        def _(v):
            ch = Chain(v, v_ch)
            v.sem_inc(y_used, 2)
            fr.vector(v, 0)
            v.wait_ge(w_in, 16 * loads)

            def body(i, more):
                ch.start(10 * i)
                for u in (0, 1):
                    v.wait_ge(q_mm, nth(i, u))
                    for c in range(C):
                        v.tensor_tensor(qk[:, u, 0, c], T1[u][:, c], bqk[:, 0], ALU.add)
                    v.wait_ge(k_mm, nth(i, u))
                    for c in range(C):
                        last = v.tensor_tensor(qk[:, u, 1, c], T2[u][:, c], bqk[:, 1], ALU.add)
                    ch.link(last)
                    v.tensor_scalar(ex[:, u], qk[:, u], 0.0, None, ALU.min).then_inc(mn_rdy, 1)
                for u in (0, 1):
                    v.wait_ge(ex_rdy, nth(i, u))
                    last = v.scalar_tensor_tensor(qk[:, u], qk[:, u], 0.0, ex[:, u], ALU.max, ALU.add)
                    last.then_inc(qk_rdy, 1)
                    v.wait_ge(qk_rdy, nth(i, u))
                    ch.link(v.tensor_tensor(prod[:, u], qk[:, u, 0], qk[:, u, 1], ALU.mult))
                    ch.link(v.tensor_reduce(den[:, u], prod[:, u].rearrange("p c (h k) -> p (c h) k", k=KD), AX.X, ALU.add))
                    ch.link(v.tensor_scalar(den[:, u], den[:, u], 1e-6, None, ALU.add))
                    ch.link(v.reciprocal(den[:, u], den[:, u]))
                    v.wait_ge(s_mm, nth(i, u))
                    for c in range(C):
                        last = v.tensor_tensor(sm[:, u, c].rearrange("p (h k) -> p h k", k=KD),
                                               T1[u][:, c, 0:P].rearrange("p (h k) -> p h k", k=KD),
                                               own[:].unsqueeze(2).broadcast_to([P, 8, KD]), ALU.mult)
                    last.then_inc(s_rdy, 1)
                if more:
                    fr.vector(v, i + 1)
                for u in (0, 1):
                    v.wait_ge(o_mm, nth(i, u))
                    v.tensor_tensor(on[:, u].rearrange("p c (h k) -> p (c h) k", k=KD),
                                    T2[u].rearrange("p c (h k) -> p (c h) k", k=KD),
                                    den[:, u].rearrange("p c h -> p (c h)").unsqueeze(2).broadcast_to([P, C * H, KD]),
                                    ALU.mult).then_inc(on_rdy, 1)
                for u in (0, 1):
                    b = 2 * i + u
                    v.wait_ge(y_mm, nth(i, u))
                    for c in range(C):
                        last = v.tensor_tensor(y[:, u, c], T1[u][:, c], bo[:], ALU.add)
                    last.then_inc(y_used, 1)
                    v.wait_ge(y_used, nth(i, u) + 2)
                    v.scalar_tensor_tensor(env.x[:, b], y[:, u], env.tg[:, 3:4], env.x[:, b], ALU.mult, ALU.add)
                ch.end(10)
            passes(v, body)

        @block.scalar
        def _(a):
            fr.scalar(a, 0)
            a.wait_ge(w_in, 16 * loads)

            def body(i, more):
                for u in (0, 1):
                    a.wait_ge(v_mm, nth(i, u))
                    for c in range(C):
                        last = a.activation(vT[:, u, c], T3[u][:, c], ACT.Identity, bias=bv[:, c:c + 1])
                    last.then_inc(v_rdy, 1)
                for u in (0, 1):
                    a.wait_ge(mn_rdy, nth(i, u))
                    a.activation(ex[:, u], ex[:, u], ACT.Exp).then_inc(ex_rdy, 1)
                for u in (0, 1):
                    a.wait_ge(oT_mm, nth(i, u))
                    a.activation(onT[:, u], T3[u], ACT.Copy).then_inc(oT_rdy, 1)
                if more:
                    fr.scalar(a, i + 1)
            passes(a, body)

        @block.tensor
        def _(pe):
            fr.tensor(pe, 0)
            pe.wait_ge(w_in, 16 * loads)

            def body(i, more):
                for u in (0, 1):
                    pe.wait_ge(fr.xnT_rdy, nth(i, u))
                    pe.wait_ge(y_used, nth(i, u))
                    product(pe, lambda m: T1[u][:, m], lambda k, m: fr.xnT[:, u, k, chunk(m)],
                            lambda k: wq[:, k]).then_inc(q_mm, 1)
                    pe.wait_ge(cT_rdy, nth(i, u))
                    product(pe, lambda m: T2[u][:, m], lambda k, m: cT[:, u, k, chunk(m)],
                            lambda k: wk[:, k]).then_inc(k_mm, 1)
                    product(pe, lambda m: T3[u][:, m], lambda k, m: wv[:, k, chunk(m)],
                            lambda k: cT[:, u, k]).then_inc(v_mm, 1)
                for u in (0, 1):
                    pe.wait_ge(qk_rdy, nth(i, u))
                    for c in range(C):
                        for tc in range(C):
                            last = pe.matmul(T1[u][:, c, 0:P], qk[:, u, 1, tc, chunk(c)], qk[:, u, 0, tc, chunk(c)],
                                             start=(tc == 0), stop=(tc == C - 1))
                    last.then_inc(s_mm, 1)
                for u in (0, 1):
                    pe.wait_ge(s_rdy, nth(i, u))
                    pe.wait_ge(v_rdy, nth(i, u))
                    for tc in range(C):
                        for c in range(C):
                            last = pe.matmul(T2[u][:, tc, chunk(c)], vT[:, u, c, chunk(tc)], sm[:, u, c],
                                             start=True, stop=True)
                    last.then_inc(o_mm, 1)
                for u in (0, 1):
                    pe.wait_ge(on_rdy, nth(i, u))
                    transpose4(pe, T3[u], on[:, u], env.ident[:]).then_inc(oT_mm, 1)
                for u in (0, 1):
                    pe.wait_ge(oT_rdy, nth(i, u))
                    product(pe, lambda m: T1[u][:, m], lambda k, m: onT[:, u, k, chunk(m)],
                            lambda k: wo[:, k]).then_inc(y_mm, 1)
                if more:
                    fr.tensor(pe, i + 1)
            passes(pe, body)



def layer3_experts(nc, env, w, sem_):
    E, F = 8, 1024
    FC = F // P
    with ExitStack() as ctx:
        sb = lambda n, s, d=F32: ctx.enter_context(nc.sbuf_tensor("E3" + n, s, d))
        w1, w2 = sb("w1", [P, 2, C, F]), sb("w2", [P, 2, FC, D])
        wr, first = sb("wr", [P, C, E]), sb("first", [P, E, E])
        xn = sb("xn", [P, C, D])
        xnT, hT = env.n2T, sb("hT", [P, 2, FC, S])
        xl, absorb = sb("xl", [P, C, S]), sb("absorb", [P, 1])
        lg, eq, seen, hot = sb("lg", [P, C, E]), sb("eq", [P, C, E]), sb("seen", [P, E, E]), sb("hot", [P, C, E])
        top, gap, ex = sb("top", [P, C, 8]), sb("gap", [P, C]), sb("ex", [P, C])
        wt = sb("wt", [P, B, C, E])
        st, mv, rstd = sb("st", [P, C, 6]), sb("mv", [P, C, 2]), sb("rstd", [P, C])
        e_in = [sem_(f"e3_in{k}") for k in range(2)]
        (w_in, st_rdy, rstd_rdy, xn_rdy, xnT_mm, xnT_rdy, lg_mm, gap_rdy, ex_rdy, h_mm, h_free,
         xl_rdy, y_mm, y_used, v_ch, g_ch) = (
            sem_("e3_" + n) for n in ("w_in", "st_rdy", "rstd_rdy", "xn_rdy", "xnT_mm", "xnT_rdy", "lg_mm", "gap_rdy",
                                      "ex_rdy", "h_mm", "h_free", "xl_rdy", "y_mm", "y_used",
                                      "v_ch", "g_ch"))
        bank = env.bank
        block = ctx.enter_context(nc.Block())

        @block.sync
        def _(sp):
            sp.dma_start(wr[:], w["L3_ffn_Wr"].rearrange("(k p) n -> p k n", p=P)).then_inc(w_in, 16)
            sp.dma_start(first[:], w["first"]).then_inc(w_in, 16)

            def load(e, k):
                at = bass.ds(e, 1)
                sp.dma_start(w1[:, k], w["L3_ffn_W1"][at].rearrange("e (k p) f -> p (e k) f", p=P)).then_inc(e_in[k], 16)
                sp.dma_start(w2[:, k], w["L3_ffn_W2"][at].rearrange("e (k p) f -> p (e k) f", p=P)).then_inc(e_in[k], 16)
            load(0, 0)
            load(1, 1)
            with sp.Fori(1, E // 2) as i:
                for k in range(2):
                    sp.wait_ge(y_mm, B * (2 * i + k - 1))
                    load(2 * i + k, k)

        @block.gpsimd
        def _(g):
            ch = Chain(g, g_ch)
            with g.Fori(0, B) as b:
                ch.start(b)
                g.wait_ge(st_rdy, b + 1)
                ln_rstd(g, ch, mv, rstd, env.mhalf, env.eps5).then_inc(rstd_rdy, 1)

        @block.vector
        def _(v):
            ch = Chain(v, v_ch)
            v.sem_inc(y_used, 2)
            v.wait_ge(w_in, 32)
            with v.Fori(0, B) as b:
                ch.start(12 * b)
                ln_stats(v, ch, env.x[:, b], st, mv, env.scrap).then_inc(st_rdy, 1)
                v.wait_ge(rstd_rdy, b + 1)
                ln_apply(v, xn, env.x[:, b], mv, rstd).then_inc(xn_rdy, 1)
                v.wait_ge(xl_rdy, b + 1)
                v.memset(env.scrap[:], 0.0)
                v.tensor_copy(xnT[:, b], xl[:]).then_inc(xnT_rdy, 1)
                v.wait_ge(lg_mm, b + 1)
                ch.link(v.tensor_copy(lg[:], bank(1)[:, :, 0:E]))
                v.memset(env.scrap[:], 0.0)
                for c in range(C):
                    last = v.max(top[:, c], lg[:, c])
                ch.link(last)
                v.tensor_tensor(gap[:], top[:, :, 1], top[:, :, 0], ALU.subtract).then_inc(gap_rdy, 1)
                for c in range(C):
                    last = v.tensor_scalar(eq[:, c], lg[:, c], top[:, c, 0:1], None, ALU.is_equal)
                ch.link(last)
                for c in range(C):
                    ch.link(v.tensor_tensor(seen[:], first[:], eq[:, c].unsqueeze(1).broadcast_to([P, E, E]), ALU.mult))
                    ch.link(v.tensor_reduce(hot[:, c], seen[:], AX.X, ALU.add))
                v.wait_ge(ex_rdy, b + 1)
                ch.link(v.tensor_scalar(ex[:], ex[:], 1.0, None, ALU.add))
                ch.link(v.reciprocal(ex[:], ex[:]))
                ch.link(v.tensor_scalar(ex[:], ex[:], env.tg[:, 7:8], None, ALU.mult))
                ch.link(v.scalar_tensor_tensor(hot[:], hot[:], 0.5, eq[:], ALU.is_lt, ALU.mult))
                for c in range(C):
                    v.tensor_scalar(wt[:, b, c], hot[:, c], ex[:, c:c + 1], None, ALU.mult)
                ch.end(12)

            with v.Fori(0, E) as e:
                with v.Fori(0, NI) as i:
                    for u in (0, 1):
                        n, b = B * e + 2 * i + u, 2 * i + u
                        v.wait_ge(y_mm, n + 1)
                        for c in range(C):
                            last = v.scalar_tensor_tensor(env.x[:, b, c], bank(6 + u)[:, c], wt[:, b, c, bass.ds(e, 1)],
                                                          env.x[:, b, c], ALU.mult, ALU.add)
                        last.then_inc(y_used, 1)

        @block.scalar
        def _(a):
            a.sem_inc(h_free, 4)
            with a.Fori(0, B) as b:
                a.wait_ge(xnT_mm, b + 1)
                a.activation(xl[:], bank(0), ACT.Copy).then_inc(xl_rdy, 1)
                a.wait_ge(gap_rdy, b + 1)
                a.activation(ex[:], gap[:], ACT.Exp).then_inc(ex_rdy, 1)
            with a.Fori(0, E * NI) as i:
                for q in range(FC // C):
                    for u in (0, 1):
                        a.wait_ge(h_mm, 8 * i + 2 * q + u + 1)
                        a.activation(hT[:, u, C * q:C * q + C], bank(2 + u + 2 * (q % 2)), ACT.Gelu).then_inc(h_free, 1)

        @block.tensor
        def _(pe):
            pe.wait_ge(w_in, 32)
            with pe.Fori(0, B) as b:
                pe.wait_ge(xn_rdy, b + 1)
                transpose4(pe, bank(0), xn, env.ident[:]).then_inc(xnT_mm, 1)
                pe.wait_ge(xl_rdy, b + 1)
                for tc in range(C):
                    for k in range(C):
                        last = pe.matmul(bank(1)[:, tc, 0:E], xl[:, k, chunk(tc)], wr[:, k], start=(k == 0), stop=(k == C - 1))
                last.then_inc(lg_mm, 1)
            pe.wait_ge(xnT_rdy, B)

            def part(n, i, k, q):
                for u in (0, 1):
                    pe.wait_ge(h_free, 8 * n + 2 * q + u + 1)
                    for c in range(C):
                        for kk in range(C):
                            last = pe.matmul(bank(2 + u + 2 * (q % 2))[:, c], w1[:, k, kk, chunk(C * q + c)],
                                             xnT[:, 2 * i + u, kk], start=(kk == 0), stop=(kk == C - 1))
                    last.then_inc(h_mm, 1)

            with pe.Fori(0, E // 2) as ee:
                for k in range(2):
                    with pe.Fori(0, NI) as i:
                        pe.wait_ge(e_in[k], 32 * ee + 32)
                        n = NI * (2 * ee + k) + i
                        for q in range(FC // C):
                            part(n, i, k, q)
                        for u in (0, 1):
                            pe.wait_ge(h_free, 8 * n + 6 + u + 1 + 4)
                            pe.wait_ge(y_used, 2 * n + u + 1)
                            product(pe, lambda m: bank(6 + u)[:, m], lambda f, m: hT[:, u, f, chunk(m)],
                                    lambda f: w2[:, k, f], K=FC).then_inc(y_mm, 1)


def store(nc, env, w, sem_):
    with ExitStack() as ctx:
        stored = sem_("stored")
        block = ctx.enter_context(nc.Block())

        @block.sync
        def _(sp):
            sp.dma_start(w["out"].rearrange("b (c p) d -> p b c d", p=P), env.x[:]).then_inc(stored, 16)
            sp.wait_ge(stored, 16)


STAGES = (prepare, layer0_attention, layer0_mha, layer0_experts, layer1_attention, layer1_experts,
          layer2_attention, layer2_experts, layer3_attention, layer3_experts)


def build(nc, w):
    with ExitStack() as ctx:
        env = Env()
        env.x = ctx.enter_context(nc.sbuf_tensor("x_all", [P, B, C, D], F32))
        env.ctxT = ctx.enter_context(nc.sbuf_tensor("ctxT_all", [P, B, C, S], F32))
        env.ident = ctx.enter_context(nc.sbuf_tensor("ident", [P, P], F32))
        env.mhalf = ctx.enter_context(nc.sbuf_tensor("mhalf", [P, 32], F32))
        env.scrap = ctx.enter_context(nc.sbuf_tensor("scrap", [P, 1], F32))
        env.eps5 = ctx.enter_context(nc.sbuf_tensor("eps5", [P, C], F32))
        env.eps6 = ctx.enter_context(nc.sbuf_tensor("eps6", [P, C], F32))
        env.tg = ctx.enter_context(nc.sbuf_tensor("tg", [P, 8], F32))
        env.n2T = ctx.enter_context(nc.sbuf_tensor("n2T_all", [P, B, C, S], F32))
        env.pick_w = ctx.enter_context(nc.sbuf_tensor("pick_w", [P, B, 2], F32))
        env.pick = ctx.enter_context(nc.sbuf_tensor("pick", [P, B, 2], U32))
        ps = ctx.enter_context(nc.psum_tensor("banks", [P, 8, 512], F32))
        env.ps = ps
        env.bank = lambda j: ps[:, j, :].rearrange("p (c d) -> p c d", c=C)
        for stage in STAGES + (store,):
            used = []

            def sem_(name):
                used.append(nc.alloc_semaphore(name))
                return used[-1]

            stage(nc, env, w, sem_)
            nc.clear_and_free_semaphores(used)
            nc.all_engine_barrier()


def dft():
    import numpy as np
    t = np.arange(S, dtype=np.float64)
    a = 2 * np.pi * np.outer(t, np.arange(P)) / S
    f = np.concatenate([np.cos(a), -np.sin(a)], axis=1)
    f[:, P] = np.cos(np.pi * t)
    g = 2 * f.T.copy() / S
    g[0] /= 2
    g[P] /= 2
    return f.astype(np.float32), g.astype(np.float32)


def shape_constants():
    import numpy as np
    f, g = dft()
    p = np.arange(P)
    r = np.arange(16)
    rot = ((p[:, None, None] - r[None, :, None]) % 16 == r[None, None, :]).astype(np.float32)
    own = (p[:, None] // 16 == np.arange(8)[None, :]).astype(np.float32)
    first = np.broadcast_to((r[None, :8] < r[:8, None]).astype(np.float32), (P, 8, 8)).copy()
    inner = np.stack([(p > 0), (p == 0)], axis=1).astype(np.float32)
    return {"dft_f": f, "dft_g": g, "rot": rot, "own": own, "first": first, "inner": inner}


COLUMNS = ("L0_xattn_bq", "L0_xattn_bk", "L0_ffn_ln1_g", "L0_ffn_ln1_b", "L0_ffn_ln2_g", "L0_ffn_ln2_b",
           "L0_ffn_mha_bq", "L0_ffn_mha_bk", "L2_ffn_ln_g", "L2_ffn_ln_b", "L2_ffn_attn_b", "L2_ffn_b1",
           "L2_ffn_b2", "L3_xattn_bv")


def kernel(**inputs):
    import numpy as np
    import concourse.bacc as bacc
    from concourse.bass_utils import run_bass_kernel_spmd

    nc = bacc.Bacc("TRN2", target_bir_lowering=False, num_devices=1)
    arrays, w = {}, {}
    given = {k: np.ascontiguousarray(a) for k, a in inputs.items()}
    given["mask_BxS2_bk0"] = np.repeat(given["mask_BxS2_bk0"], 4, axis=1).view(np.int32)
    for name in COLUMNS:
        given[name] = np.ascontiguousarray(given[name].reshape(-1, P).T)
    for name, a in {**given, **shape_constants()}.items():
        arrays[f"in_{name}_dram"] = a
        w[name] = nc.dram_tensor(f"in_{name}_dram", a.shape, mybir.dt.from_np(a.dtype),
                                 kind="ExternalInput").ap()
    w["out"] = nc.dram_tensor("out_dram", (B, S, D), F32, kind="ExternalOutput").ap()
    build(nc, w)
    r = run_bass_kernel_spmd(nc, [arrays], core_ids=[0])
    return r.results[0]["out_dram"]
```
